# Optimizing a Trainium2 kernel written in Bass

```python
import numpy as np
import jax
import jax.numpy as jnp

def _softmax(x, axis=-1):
    return jax.nn.softmax(x, axis=axis)

def _gelu(x):
    return jax.nn.gelu(x, approximate=True)

def _silu(x):
    return jax.nn.silu(x)

def _sigmoid(x):
    return jax.nn.sigmoid(x)

def _layernorm(x, axis=-1, eps=1e-05):
    m = jnp.mean(x, axis=axis, keepdims=True)
    v = jnp.var(x, axis=axis, keepdims=True)
    return (x - m) / jnp.sqrt(v + eps)

def _scatter_add(tgt, idx, src, axis=0):
    return tgt.at[idx].add(src)

def _segment_sum(src, seg, n):
    return jax.ops.segment_sum(src, seg, n)
kernel_name = 'mk_gnn_resnorm_d1_gnn_r64_bde240'

def setup_inputs(seed: int=0):
    np.random.seed(seed)
    _w = jnp.asarray

    def _rec_inputs():
        import jax
        import jax.numpy as jnp
        _gk = jax.random.key(seed)
        x = -0.0005121 + 1.001 * jax.random.normal(jax.random.fold_in(_gk, 1), (100000, 64), jnp.float32)
        src = jax.random.randint(jax.random.fold_in(_gk, 2), (50000,), 0, 100000, jnp.int32)
        dst = jax.random.randint(jax.random.fold_in(_gk, 3), (50000,), 0, 100000, jnp.int32)
        _o = jnp.argsort(dst, stable=True)
        src = src[_o]
        dst = dst[_o]
        edge_attr_64 = -9.77346e-05 + 0.999888 * jax.random.normal(jax.random.fold_in(_gk, 12), (50000, 64), jnp.float32)
        return (x, src, dst, edge_attr_64)
    x, src, dst, edge_attr_64 = _rec_inputs()

    def _L0_gnn_setup():
        import jax, jax.numpy as jnp
        import numpy as np
        N_NODES = 50000
        N_EDGES = 12500
        D = 64
        H = 128
        key = jax.random.key(seed)
        ks = jax.random.split(key, 8)
        s = 0.05
        return {'nodes': jax.random.normal(ks[0], (N_NODES, D), jnp.float32), 'edges': jax.random.normal(ks[1], (N_EDGES, D), jnp.float32), 'We1': jax.random.normal(ks[2], (3 * D, H), jnp.float32) * s, 'be1': jnp.zeros((H,), jnp.float32), 'We2': jax.random.normal(ks[3], (H, D), jnp.float32) * s, 'be2': jnp.zeros((D,), jnp.float32), 'Wn1': jax.random.normal(ks[4], (2 * D, H), jnp.float32) * s, 'bn1': jnp.zeros((H,), jnp.float32), 'Wn2': jax.random.normal(ks[5], (H, D), jnp.float32) * s, 'bn2': jnp.zeros((D,), jnp.float32), 'senders': jax.random.randint(ks[6], (N_EDGES,), 0, N_NODES, jnp.int32), 'receivers': jax.random.randint(ks[7], (N_EDGES,), 0, N_NODES, jnp.int32)}
    _L0_gnn_all = _L0_gnn_setup()
    _L0_gnn_in = {k: v for k, v in _L0_gnn_all.items() if k in ('We1', 'be1', 'We2', 'be2', 'Wn1', 'bn1', 'Wn2', 'bn2')}
    del _L0_gnn_all
    return {'x': x, 'src': src, 'dst': dst, 'edge_attr_64': edge_attr_64, 'L0_gnn_We1': _L0_gnn_in['We1'], 'L0_gnn_be1': _L0_gnn_in['be1'], 'L0_gnn_We2': _L0_gnn_in['We2'], 'L0_gnn_be2': _L0_gnn_in['be2'], 'L0_gnn_Wn1': _L0_gnn_in['Wn1'], 'L0_gnn_bn1': _L0_gnn_in['bn1'], 'L0_gnn_Wn2': _L0_gnn_in['Wn2'], 'L0_gnn_bn2': _L0_gnn_in['bn2']}

def reference(x, src, dst, edge_attr_64, L0_gnn_We1, L0_gnn_be1, L0_gnn_We2, L0_gnn_be2, L0_gnn_Wn1, L0_gnn_bn1, L0_gnn_Wn2, L0_gnn_bn2):
    import jax
    import jax.numpy as jnp

    def _L0_gnn_ref(nodes, edges, We1, be1, We2, be2, Wn1, bn1, Wn2, bn2, senders, receivers):
        import jax, jax.numpy as jnp
        import numpy as np
        N_NODES = 50000
        N_EDGES = 12500
        D = 64
        H = 128
        edge_in = jnp.concatenate([edges, nodes[receivers], nodes[senders]], axis=-1)
        h = jax.nn.relu(edge_in @ We1 + be1)
        new_edges = h @ We2 + be2
        agg = jax.ops.segment_sum(new_edges, receivers, num_segments=nodes.shape[0])
        node_in = jnp.concatenate([agg, nodes], axis=-1)
        h2 = jax.nn.relu(node_in @ Wn1 + bn1)
        new_nodes = h2 @ Wn2 + bn2
        return new_nodes
    x = _layernorm(x + _L0_gnn_ref(x, edge_attr_64, L0_gnn_We1, L0_gnn_be1, L0_gnn_We2, L0_gnn_be2, L0_gnn_Wn1, L0_gnn_bn1, L0_gnn_Wn2, L0_gnn_bn2, src, dst), axis=-1)
    return x

_drawn_inputs = setup_inputs


def setup_inputs(seed=0):
    import zlib

    import numpy as np

    out = dict(_drawn_inputs(seed))
    spreads = {'L0_gnn_be1': (0.0, 0.8),
     'L0_gnn_be2': (0.0, 0.646),
     'L0_gnn_bn1': (0.0, 0.1),
     'L0_gnn_bn2': (0.0, 0.1)}
    factors = {'edge_attr_64': 3.648}
    for name, (base, spread) in spreads.items():
        noise = np.random.default_rng([zlib.crc32(name.encode()), seed]).standard_normal(out[name].shape)
        drawn = base * np.exp(spread * noise) if base else spread * noise
        out[name] = jnp.asarray(drawn.astype(out[name].dtype))
    for name, factor in factors.items():
        out[name] = (out[name] * factor).astype(out[name].dtype)
    return out
```

```python
from contextlib import ExitStack

import concourse.bass as bass
from concourse import mybir

P = 128
F32 = mybir.dt.float32
I32 = mybir.dt.int32
ALU = mybir.AluOpType
ACT = mybir.ActivationFunctionType

U = 4
GROUP = U * P
EPS = 1e-5


def gnn_resnorm(nc, x, src, dst, edges, we1, be1, we2, be2, wn1, bn1, wn2, bn2, out):
    N, D = x.shape
    E = src.shape[0]
    H = we1.shape[1]
    REC = D + 2
    EG = -(-E // GROUP)
    ETAIL = (E - (EG - 1) * GROUP) // U
    NG = -(-N // GROUP)
    NTAIL = (N - (NG - 1) * GROUP) // U
    assert D == 64 and H == P and EG % 2 == 0 and NG % 2 == 0
    assert (EG - 1) * GROUP + ETAIL * U == E and (NG - 1) * GROUP + NTAIL * U == N
    EPAIRS, NPAIRS = EG // 2, NG // 2

    messages = nc.dram_tensor("messages", [EG * GROUP, REC], F32, kind="Internal").ap()
    sums = nc.dram_tensor("sums", [N + P, D], F32, kind="Internal").ap()
    ZPARTS = 12
    ZCOLS = (N + P) * D // P // ZPARTS
    assert ZCOLS * P * ZPARTS == (N + P) * D
    sums_flat = sums.rearrange("n d -> (n d)").rearrange("(p z c) -> p z c", p=P, z=ZPARTS)

    def rows(t, g, n, width):
        return t[bass.ds(g * GROUP, n * U), :].rearrange("(p u) d -> p (u d)", u=U)

    def ids(t, g, n):
        return t[bass.ds(g * GROUP, n * U)].rearrange("(p u) -> p u", u=U)

    with ExitStack() as ctx:
        def sb(name, shape, dt=F32):
            return ctx.enter_context(nc.sbuf_tensor(name, shape, dt))

        def ps(name, shape):
            return ctx.enter_context(nc.psum_tensor(name, shape, F32))

        def sem(name):
            return ctx.enter_context(nc.semaphore(name))

        zeros = sb("zeros", [P, ZCOLS])
        ident = sb("ident", [P, P])
        earlier = sb("earlier", [P, P])
        spare = sb("spare", [P, 1])
        eps = sb("eps", [P, 1])
        we1_er = sb("we1_er", [P, H])
        we1_s = sb("we1_s", [P, 2, H])
        we2_sb = sb("we2_sb", [P, D])
        wn1_sb = sb("wn1_sb", [P, H])
        wn2_sb = sb("wn2_sb", [P, D])
        be1_c = sb("be1_c", [P, 1])
        bn1_c = sb("bn1_c", [P, 1])
        be2_b = sb("be2_b", [P, D])
        bn2_b = sb("bn2_b", [P, D])
        src_id = sb("src_id", [P, 2, U], I32)
        dst_id = sb("dst_id", [P, 2, U], I32)
        edge_recv = sb("edge_recv", [P, 2, U, 2 * D])
        sender = sb("sender", [P, 2, U * D])
        edge_recv_t = sb("edge_recv_t", [P, 2, U * P])
        sender_t = sb("sender_t", [P, 2, 2 * P])
        ehid = sb("ehid", [P, 2, U * P])
        rec = sb("rec", [P, 2, U, REC])
        recin = sb("recin", [P, 2, U, REC])
        same = sb("same", [P, 2, P])
        same_earlier = sb("same_earlier", [P, P])
        n_earlier = sb("n_earlier", [P, 2])
        is_later = sb("is_later", [P, 2])
        to_spare = sb("to_spare", [P, 2])
        row_id = sb("row_id", [P, 2], I32)
        summed = sb("summed", [P, 2, D])
        xt = sb("xt", [P, 2, (U + 1) * D])
        aggt = sb("aggt", [P, 2, U * D])
        node_t = sb("node_t", [P, 2, U * P])
        nhid = sb("nhid", [P, 2, U * P])
        y = sb("y", [P, 2, U, D])
        stats = sb("stats", [P, 2, U, 6])
        meanvar = sb("meanvar", [P, 2, U, 2])
        std = sb("std", [P, 2, U])
        rstd = sb("rstd", [P, 2, U])
        res = sb("res", [P, 2, U, D])

        ps_er = ps("ps_er", [P, U * P])
        ps_s = ps("ps_s", [P, 512])
        ps_eh = ps("ps_eh", [P, U * P])
        ps_msg = ps("ps_msg", [P, 512])
        ps_node = ps("ps_node", [P, U * P])
        ps_nh = ps("ps_nh", [P, U * P])
        ps_new = ps("ps_new", [P, 512])
        ps_ids = ps_s[:, 0:P]
        ps_sum = ps_msg[:, 0:D]

        s_weights = sem("s_weights")
        s_const = sem("s_const")
        s_const2 = sem("s_const2")
        s_halves = sem("s_halves")
        s_zeroed = sem("s_zeroed")
        ids_in = [sem(f"ids_in{i}") for i in range(2)]
        edges_in = [sem(f"edges_in{i}") for i in range(2)]
        gathered = [sem(f"gathered{i}") for i in range(2)]
        rec_out = [sem(f"rec_out{i}") for i in range(2)]
        dst_noted = sem("dst_noted")
        e_turned = sem("e_turned")
        er_copied = sem("er_copied")
        s_copied = sem("s_copied")
        e_hidden = sem("e_hidden")
        e_relu = sem("e_relu")
        e_msg = sem("e_msg")
        rec_made = sem("rec_made")
        rec_in = [sem(f"rec_in{i}") for i in range(2)]
        ids_spread = sem("ids_spread")
        same_made = sem("same_made")
        counted = sem("counted")
        later_made = sem("later_made")
        spare_made = sem("spare_made")
        row_made = sem("row_made")
        sum_made = sem("sum_made")
        sum_copied = sem("sum_copied")
        scattered = sem("scattered")
        pool_passed = sem("pool_passed")
        dve_passed = sem("dve_passed")
        x_in = [sem(f"x_in{i}") for i in range(2)]
        res_out = [sem(f"res_out{i}") for i in range(2)]
        n_turned = sem("n_turned")
        node_copied = sem("node_copied")
        n_hidden = sem("n_hidden")
        n_relu = sem("n_relu")
        n_new = sem("n_new")
        n_added = sem("n_added")
        n_biased = sem("n_biased")
        n_stats = sem("n_stats")
        n_aggr = sem("n_aggr")
        n_std = sem("n_std")
        n_rstd = sem("n_rstd")
        n_normed = sem("n_normed")

        NWEIGHTS = 10
        block = ctx.enter_context(nc.Block())

        def pairs(eng, count, step):
            step(0, True, False)
            with eng.Fori(1, count - 1) as i:
                step(i, False, False)
            step(count - 1, False, True)

        def eparts(last, s):
            return ETAIL if last and s == 1 else P

        def nparts(last, s):
            return NTAIL if last and s == 1 else P

        def cols(t, n):
            return t.rearrange("p (u r) -> p u r", u=U)[:, :, 0:n]

        @block.sync
        def _(sp):
            for w, a in ((we1_er[:, :], we1[0:2 * D, :]), (we1_s[0:D, 0, :], we1[2 * D:3 * D, :]),
                         (we1_s[D:2 * D, 1, :], we1[2 * D:3 * D, :]), (we2_sb[:, :], we2), (wn1_sb[:, :], wn1),
                         (wn2_sb[:, :], wn2), (be1_c[:, :], be1.rearrange("(h o) -> h o", o=1)),
                         (bn1_c[:, :], bn1.rearrange("(h o) -> h o", o=1)),
                         (be2_b[:, :], be2.rearrange("(a d) -> a d", a=1).to_broadcast([P, D])),
                         (bn2_b[:, :], bn2.rearrange("(a d) -> a d", a=1).to_broadcast([P, D]))):
                sp.dma_start(w, a).then_inc(s_weights, 16)

            def load_edges(i, first, s, n):
                g = 2 * i + s
                if not first:
                    sp.wait_ge(gathered[s], 2 * U * 16 * i)
                    sp.wait_ge(dst_noted, g - 1)
                sp.dma_start(src_id[0:n, s, :], ids(src, g, n)).then_inc(ids_in[s], 16)
                sp.dma_start(dst_id[0:n, s, :], ids(dst, g, n)).then_inc(ids_in[s], 16)
                if not first:
                    sp.wait_ge(e_turned, g - 1)
                sp.dma_start(edge_recv[0:n, s, :, 0:D],
                             edges[bass.ds(g * GROUP, n * U), :].rearrange("(p u) d -> p u d", u=U))\
                  .then_inc(edges_in[s], 16)

            def store_rec(i, s, n):
                g = 2 * i + s
                sp.wait_ge(rec_made, g + 1)
                sp.dma_start(rows(messages, g, n, REC), rec[0:n, s, :, :].rearrange("p u d -> p (u d)"))\
                  .then_inc(rec_out[s], 16)

            for s in range(2):
                load_edges(0, True, s, P)
            sp.wait_ge(s_const, 1)
            for z in range(ZPARTS):
                sp.dma_start(sums_flat[:, z, :], zeros[:, :]).then_inc(s_zeroed, 16)
            with sp.Fori(0, EPAIRS - 2) as i:
                for s in range(2):
                    store_rec(i, s, P)
                    load_edges(i + 1, False, s, P)
            for s in range(2):
                store_rec(EPAIRS - 2, s, P)
                load_edges(EPAIRS - 1, False, s, eparts(True, s))
            for s in range(2):
                store_rec(EPAIRS - 1, s, eparts(True, s))
            for s in range(2):
                sp.wait_ge(rec_out[s], 16 * EPAIRS)

            def load_rec(i, first, last):
                for s in range(2):
                    g = 2 * i + s
                    n = eparts(last, s)
                    if not first:
                        sp.wait_ge(sum_made, U * (g - 1))
                        sp.wait_ge(row_made, U * (g - 1))
                    sp.dma_start(recin[0:n, s, :, :].rearrange("p u d -> p (u d)"), rows(messages, g, n, REC))\
                      .then_inc(rec_in[s], 16)

            pairs(sp, EPAIRS, load_rec)
            sp.wait_ge(scattered, 16 * U * EG)

            def load_nodes(i, first, s, n):
                g = 2 * i + s
                if not first:
                    sp.wait_ge(n_turned, g - 1)
                    sp.wait_ge(n_added, g - 1)
                sp.dma_start(xt[0:n, s, D:(U + 1) * D], rows(x, g, n, D)).then_inc(x_in[s], 16)
                sp.dma_start(aggt[0:n, s, :], rows(sums, g, n, D)).then_inc(x_in[s], 16)

            def store_nodes(i, s, n):
                g = 2 * i + s
                sp.wait_ge(n_normed, g + 1)
                sp.dma_start(rows(out, g, n, D), res[0:n, s, :, :].rearrange("p u d -> p (u d)"))\
                  .then_inc(res_out[s], 16)

            for s in range(2):
                load_nodes(0, True, s, P)
            with sp.Fori(0, NPAIRS - 2) as i:
                for s in range(2):
                    load_nodes(i + 1, False, s, P)
                    store_nodes(i, s, P)
            for s in range(2):
                load_nodes(NPAIRS - 1, False, s, nparts(True, s))
                store_nodes(NPAIRS - 2, s, P)
            for s in range(2):
                store_nodes(NPAIRS - 1, s, nparts(True, s))
            for s in range(2):
                sp.wait_ge(res_out[s], 16 * NPAIRS)

        @block.gpsimd
        def _(pool):
            pool.memset(zeros[:, :], 0.0).then_inc(s_const, 1)
            pool.memset(ident[:, :], 0.0).then_inc(s_const, 1)
            pool.memset(earlier[:, :], 1.0).then_inc(s_const, 1)
            pool.memset(eps[:, :], EPS).then_inc(s_const, 1)
            pool.memset(xt[:, :, 0:D], 0.0).then_inc(s_const, 1)
            pool.wait_ge(s_const, 5)
            pool.affine_select(out=ident[:, :], in_=ident[:, :], compare_op=ALU.not_equal, fill=1.0,
                               base=0, pattern=[[-1, P]], channel_multiplier=1).then_inc(s_const2, 1)
            pool.affine_select(out=earlier[:, :], in_=earlier[:, :], compare_op=ALU.is_gt, fill=0.0,
                               base=0, pattern=[[-1, P]], channel_multiplier=1).then_inc(s_const2, 1)
            pool.iota(row_id[:, 0:1], pattern=[[0, 1]], base=N, channel_multiplier=1).then_inc(s_const2, 1)
            pool.wait_ge(s_const2, 3)
            pool.tensor_copy(spare[:, :], row_id[:, 0:1]).then_inc(s_const2, 1)

            def gather(i, first, last):
                for s in range(2):
                    g = 2 * i + s
                    n = eparts(last, s)
                    pool.wait_ge(ids_in[s], 32 * i + 32)
                    if not first:
                        pool.wait_ge(e_turned, g - 1)
                    pool.sem_inc(pool_passed, 1)
                    for u in range(U):
                        pool.indirect_dma_start(
                            out=edge_recv[0:n, s, u, D:2 * D], out_offset=None, in_=x,
                            in_offset=bass.IndirectOffsetOnAxis(ap=dst_id[0:n, s, u:u + 1], axis=0))\
                            .then_inc(gathered[s], 16)
                        pool.indirect_dma_start(
                            out=sender[0:n, s, u * D:(u + 1) * D], out_offset=None, in_=x,
                            in_offset=bass.IndirectOffsetOnAxis(ap=src_id[0:n, s, u:u + 1], axis=0))\
                            .then_inc(gathered[s], 16)

            pairs(pool, EPAIRS, gather)
            pool.wait_ge(s_zeroed, 16 * ZPARTS)

            def scatter(i, first, last):
                for s in range(2):
                    n = eparts(last, s)
                    for u in range(U):
                        k = U * (2 * i + s) + u
                        pool.wait_ge(row_made, k + 1)
                        pool.wait_ge(sum_copied, k + 1)
                        if not (first and s == 0 and u == 0):
                            pool.wait_ge(scattered, 16 * k)
                        pool.sem_inc(pool_passed, 1)
                        pool.indirect_dma_start(
                            out=sums, out_offset=bass.IndirectOffsetOnAxis(ap=row_id[0:n, u % 2:u % 2 + 1], axis=0),
                            in_=summed[0:n, u % 2, :], in_offset=None, compute_op=ALU.add)\
                            .then_inc(scattered, 16)

            pairs(pool, EPAIRS, scatter)

        @block.tensor
        def _(pe):
            pe.wait_ge(s_const2, 2)
            pe.wait_ge(s_halves, 2)
            pe.wait_ge(s_weights, 16 * NWEIGHTS)

            def edge_group(i, first, last):
                for s in range(2):
                    g = 2 * i + s
                    n = eparts(last, s)
                    began = not (first and s == 0)
                    pe.wait_ge(edges_in[s], 16 * i + 16)
                    pe.wait_ge(gathered[s], 2 * U * 16 * (i + 1))
                    if began:
                        pe.wait_ge(er_copied, g)
                        pe.wait_ge(s_copied, g)
                    for u in range(U):
                        pe.transpose(ps_er[:, u * P:u * P + n], edge_recv[0:n, s, u, :], ident[0:n, 0:n])
                    for v in range(2):
                        last_t = pe.transpose(ps_s[:, v * P:v * P + n], sender[0:n, s, v * P:(v + 1) * P],
                                              ident[0:n, 0:n])
                    last_t.then_inc(e_turned, 1)
                    pe.wait_ge(er_copied, g + 1)
                    pe.wait_ge(s_copied, g + 1)
                    if began:
                        pe.wait_ge(e_relu, g)
                    pe.matmul(cols(ps_eh[:, :], n), we1_er[:, :], cols(edge_recv_t[:, s, :], n),
                              start=True, stop=False)
                    for h in range(2):
                        mm = pe.matmul(ps_eh[:, :].rearrange("p (v h r) -> p h v r", v=2, h=2)[:, h, :, 0:n],
                                       we1_s[:, h, :],
                                       sender_t[:, s, :].rearrange("p (v r) -> p v r", v=2)[:, :, 0:n],
                                       start=False, stop=(h == 1))
                    mm.then_inc(e_hidden, 1)
                    pe.wait_ge(e_relu, g + 1)
                    if began:
                        pe.wait_ge(rec_made, g)
                    for u in range(U):
                        mm = pe.matmul(ps_msg[0:n, u * D:(u + 1) * D], ehid[:, s, u * P:u * P + n], we2_sb[:, :],
                                       start=True, stop=True)
                    mm.then_inc(e_msg, 1)

            pairs(pe, EPAIRS, edge_group)

            def sum_group(i, first, last):
                for s in range(2):
                    n = eparts(last, s)
                    pe.wait_ge(rec_in[s], 16 * i + 16)
                    for u in range(U):
                        k = U * (2 * i + s) + u
                        began = not (first and s == 0 and u == 0)
                        if began:
                            pe.wait_ge(same_made, k)
                        pe.matmul(ps_ids[:, 0:n], recin[0:n, s, u, D:D + 1].to_broadcast([n, P]),
                                  ident[0:n, 0:n], start=True, stop=True).then_inc(ids_spread, 1)
                        pe.wait_ge(same_made, k + 1)
                        if began:
                            pe.wait_ge(sum_copied, k)
                        pe.matmul(ps_sum[0:n, :], same[0:n, u % 2, 0:n], recin[0:n, s, u, 0:D],
                                  start=True, stop=True).then_inc(sum_made, 1)

            pairs(pe, EPAIRS, sum_group)

            def node_group(i, first, last):
                for s in range(2):
                    g = 2 * i + s
                    n = nparts(last, s)
                    began = not (first and s == 0)
                    pe.wait_ge(x_in[s], 32 * i + 32)
                    if began:
                        pe.wait_ge(node_copied, g)
                    for u in range(U):
                        pe.transpose(ps_node[:, u * P:u * P + n], xt[0:n, s, u * D:(u + 2) * D], ident[0:n, 0:n])
                    for u in range(U):
                        t = pe.transpose(ps_node[0:D, u * P:u * P + n], aggt[0:n, s, u * D:(u + 1) * D],
                                         ident[0:n, 0:n])
                    t.then_inc(n_turned, 1)
                    pe.wait_ge(node_copied, g + 1)
                    if began:
                        pe.wait_ge(n_relu, g)
                    mm = pe.matmul(cols(ps_nh[:, :], n), wn1_sb[:, :], cols(node_t[:, s, :], n),
                                   start=True, stop=True)
                    mm.then_inc(n_hidden, 1)
                    pe.wait_ge(n_relu, g + 1)
                    if began:
                        pe.wait_ge(n_added, g)
                    for u in range(U):
                        mm = pe.matmul(ps_new[0:n, u * D:(u + 1) * D], nhid[:, s, u * P:u * P + n], wn2_sb[:, :],
                                       start=True, stop=True)
                    mm.then_inc(n_new, 1)

            pairs(pe, NPAIRS, node_group)

        @block.scalar
        def _(act):
            act.wait_ge(s_weights, 16 * NWEIGHTS)
            act.wait_ge(s_const, 5)

            def edge_group(i, first, last):
                for s in range(2):
                    g = 2 * i + s
                    n = eparts(last, s)
                    act.wait_ge(e_turned, g + 1)
                    if not first:
                        act.wait_ge(e_hidden, g - 1)
                    act.activation(sender_t[:, s, :].rearrange("p (v r) -> p v r", v=2)[:, :, 0:n],
                                   ps_s[:, 0:2 * P].rearrange("p (v r) -> p v r", v=2)[:, :, 0:n], ACT.Copy)\
                       .then_inc(s_copied, 1)
                    act.wait_ge(e_hidden, g + 1)
                    if not first:
                        act.wait_ge(e_msg, g - 1)
                    act.activation(cols(ehid[:, s, :], n), cols(ps_eh[:, :], n), ACT.Relu, bias=be1_c[:, 0:1])\
                       .then_inc(e_relu, 1)

            pairs(act, EPAIRS, edge_group)

            def sum_group(i, first, last):
                for s in range(2):
                    n = eparts(last, s)
                    for u in range(U):
                        k = U * (2 * i + s) + u
                        act.wait_ge(sum_made, k + 1)
                        if not (first and s == 0 and u < 2):
                            act.wait_ge(scattered, 16 * (k - 1))
                        act.activation(summed[0:n, u % 2, :], ps_sum[0:n, :], ACT.Copy).then_inc(sum_copied, 1)

            pairs(act, EPAIRS, sum_group)

            def node_group(i, first, last):
                for s in range(2):
                    g = 2 * i + s
                    n = nparts(last, s)
                    act.wait_ge(n_hidden, g + 1)
                    if not first:
                        act.wait_ge(n_new, g - 1)
                    act.activation(cols(nhid[:, s, :], n), cols(ps_nh[:, :], n), ACT.Relu, bias=bn1_c[:, 0:1])\
                       .then_inc(n_relu, 1)
                    act.wait_ge(n_aggr, g + 1)
                    if not first:
                        act.wait_ge(n_rstd, g - 1)
                    act.activation(std[0:n, s, :], meanvar[0:n, s, :, 1], ACT.Sqrt, bias=eps[0:n, 0:1])\
                       .then_inc(n_std, 1)

            pairs(act, NPAIRS, node_group)

        @block.vector
        def _(dve):
            dve.memset(we1_s[D:2 * D, 0, :], 0.0).then_inc(s_halves, 1)
            dve.memset(we1_s[0:D, 1, :], 0.0).then_inc(s_halves, 1)
            dve.wait_ge(s_weights, 16 * NWEIGHTS)
            dve.wait_ge(s_const2, 4)

            def edge_group(i, first, last):
                for s in range(2):
                    g = 2 * i + s
                    n = eparts(last, s)
                    dve.wait_ge(ids_in[s], 32 * i + 32)
                    if not first:
                        dve.wait_ge(rec_out[s], 16 * i)
                    dve.tensor_copy(rec[0:n, s, :, D:D + 2], dst_id[0:n, s, :].unsqueeze(2).to_broadcast([n, U, 2]))\
                       .then_inc(dst_noted, 1)
                    dve.wait_ge(e_turned, g + 1)
                    if not first:
                        dve.wait_ge(e_hidden, g - 1)
                    dve.tensor_copy(cols(edge_recv_t[:, s, :], n), cols(ps_er[:, :], n)).then_inc(er_copied, 1)
                    dve.wait_ge(e_msg, g + 1)
                    dve.tensor_tensor(rec[0:n, s, :, 0:D], ps_msg[0:n, 0:U * D].rearrange("p (u d) -> p u d", u=U),
                                      be2_b[0:n, :].unsqueeze(1).to_broadcast([n, U, D]), ALU.add)\
                       .then_inc(rec_made, 1)

            pairs(dve, EPAIRS, edge_group)

            def sum_group(i, first, last):
                for s in range(2):
                    n = eparts(last, s)
                    for u in range(U):
                        k = U * (2 * i + s) + u
                        b = u % 2
                        began2 = not (first and s == 0 and u < 2)
                        began = not (first and s == 0 and u == 0)
                        receiver = recin[0:n, s, u, D:D + 1]
                        if u == 0:
                            dve.wait_ge(rec_in[s], 16 * i + 16)
                        dve.wait_ge(ids_spread, k + 1)
                        if began2:
                            dve.wait_ge(sum_made, k - 1)
                        dve.tensor_scalar(same[0:n, b, 0:n], ps_ids[0:n, 0:n], receiver, None, ALU.is_equal)\
                           .then_inc(same_made, 1)
                        dve.wait_ge(same_made, k + 1)
                        if began:
                            dve.wait_ge(later_made, k)
                        dve.tensor_tensor_reduce(same_earlier[0:n, 0:n], same[0:n, b, 0:n], earlier[0:n, 0:n], 1.0, 0.0,
                                                 ALU.mult, ALU.add, n_earlier[0:n, b:b + 1]).then_inc(counted, 1)
                        dve.wait_ge(counted, k + 1)
                        if began:
                            dve.wait_ge(row_made, k)
                        dve.tensor_scalar(is_later[0:n, b:b + 1], n_earlier[0:n, b:b + 1], 1.0, None, ALU.min)\
                           .then_inc(later_made, 1)
                        dve.tensor_tensor(to_spare[0:n, b:b + 1], spare[0:n, :], receiver, ALU.subtract)\
                           .then_inc(spare_made, 1)
                        dve.wait_ge(later_made, k + 1)
                        dve.wait_ge(spare_made, k + 1)
                        if began2:
                            dve.wait_ge(scattered, 16 * (k - 1))
                        dve.scalar_tensor_tensor(out=row_id[0:n, b:b + 1], in0=to_spare[0:n, b:b + 1],
                                                 scalar=is_later[0:n, b:b + 1], in1=receiver,
                                                 op0=ALU.mult, op1=ALU.add).then_inc(row_made, 1)

            pairs(dve, EPAIRS, sum_group)

            def node_group(i, first, last):
                for s in range(2):
                    g = 2 * i + s
                    n = nparts(last, s)
                    dve.wait_ge(n_turned, g + 1)
                    if not first:
                        dve.wait_ge(n_hidden, g - 1)
                    dve.tensor_copy(cols(node_t[:, s, :], n), cols(ps_node[:, :], n)).then_inc(node_copied, 1)
                    dve.wait_ge(n_new, g + 1)
                    if not first:
                        dve.wait_ge(n_normed, g - 1)
                    dve.tensor_tensor(y[0:n, s, :, :].rearrange("p u d -> p (u d)"), ps_new[0:n, 0:U * D],
                                      xt[0:n, s, D:(U + 1) * D], ALU.add).then_inc(n_added, 1)
                    dve.wait_ge(n_added, g + 1)
                    dve.tensor_tensor(y[0:n, s, :, :], y[0:n, s, :, :], bn2_b[0:n, :].unsqueeze(1).to_broadcast([n, U, D]),
                                      ALU.add).then_inc(n_biased, 1)
                    dve.wait_ge(n_biased, g + 1)
                    for u in range(U):
                        st = dve.bn_stats(stats[0:n, s, u, :], y[0:n, s, u, :])
                    st.then_inc(n_stats, 1)
                    dve.wait_ge(n_stats, g + 1)
                    if not first:
                        dve.wait_ge(n_std, g - 1)
                    dve.sem_inc(dve_passed, 1)
                    for u in range(U):
                        ag = dve.bn_aggr(meanvar[0:n, s, u, :], stats[0:n, s, u, :])
                    ag.then_inc(n_aggr, 1)
                    dve.wait_ge(n_std, g + 1)
                    dve.reciprocal(rstd[0:n, s, :], std[0:n, s, :]).then_inc(n_rstd, 1)
                    dve.wait_ge(n_rstd, g + 1)
                    if not first:
                        dve.wait_ge(res_out[s], 16 * i)
                    for u in range(U):
                        nm = dve.tensor_scalar(res[0:n, s, u, :], y[0:n, s, u, :], meanvar[0:n, s, u, 0:1],
                                               rstd[0:n, s, u:u + 1], ALU.subtract, ALU.mult)
                    nm.then_inc(n_normed, 1)

            pairs(dve, NPAIRS, node_group)


_INS = ['x', 'src', 'dst', 'edge_attr_64', 'L0_gnn_We1', 'L0_gnn_be1', 'L0_gnn_We2', 'L0_gnn_be2',
        'L0_gnn_Wn1', 'L0_gnn_bn1', 'L0_gnn_Wn2', 'L0_gnn_bn2']


def kernel(**inputs):
    import numpy as _np
    import concourse.bacc as _bacc
    from concourse import mybir as _mybir
    from concourse.bass_utils import run_bass_kernel_spmd as _run

    nc = _bacc.Bacc("TRN2", target_bir_lowering=False, num_devices=1)
    arrays, args = {}, []
    for name in _INS:
        a = _np.ascontiguousarray(inputs[name])
        arrays[f"in_{name}"] = a
        args.append(nc.dram_tensor(f"in_{name}", a.shape, _mybir.dt.from_np(a.dtype), kind="ExternalInput").ap())
    out = nc.dram_tensor("out_0", inputs['x'].shape, F32, kind="ExternalOutput").ap()
    gnn_resnorm(nc, *args, out)
    r = _run(nc, [arrays], core_ids=[0])
    return r.results[0]["out_0"]
```

```python
from contextlib import ExitStack

import concourse.bass as bass
from concourse import mybir

P = 128
F32 = mybir.dt.float32
BF16 = mybir.dt.bfloat16
AX_X = mybir.AxisListType.X
I32 = mybir.dt.int32
ALU = mybir.AluOpType
ACT = mybir.ActivationFunctionType

U = 4
GROUP = U * P
EPS = 1e-5


def gnn_resnorm(nc, x, src, dst, edges, we1, be1, we2, be2, wn1, bn1, wn2, bn2, out):
    N, D = x.shape
    E = src.shape[0]
    H = we1.shape[1]
    REC = D + 2
    EG = -(-E // GROUP)
    ETAIL = (E - (EG - 1) * GROUP) // U
    NG = -(-N // GROUP)
    NTAIL = (N - (NG - 1) * GROUP) // U
    assert D == 64 and H == P and EG % 2 == 0 and NG % 2 == 0
    assert (EG - 1) * GROUP + ETAIL * U == E and (NG - 1) * GROUP + NTAIL * U == N
    EPAIRS, NPAIRS = EG // 2, NG // 2
    BLOCK_EDGES = P
    HALF = 2 * GROUP
    BLOCKS = HALF // P
    LAG = 4
    KNOWN_GROUPS = LAG - 1
    PLAN = 32
    EROWS = 125
    ECOLS = E // EROWS
    assert EROWS * ECOLS == E and N <= PLAN * PLAN * P and NPAIRS == EG and E + P <= EG * GROUP

    starts = nc.dram_tensor("starts", [PLAN, PLAN], I32, kind="Internal").ap()
    messages = nc.dram_tensor("messages", [EG * GROUP, REC], F32, kind="Internal").ap()
    sums = nc.dram_tensor("sums", [N + P, D], F32, kind="Internal").ap()
    ZPARTS = 12
    ZCOLS = (N + P) * D // P // ZPARTS
    assert ZCOLS * P * ZPARTS == (N + P) * D
    sums_flat = sums.rearrange("n d -> (n d)").rearrange("(p z c) -> p z c", p=P, z=ZPARTS)

    def rows(t, g, n, width):
        return t[bass.ds(g * GROUP, n * U), :].rearrange("(p u) d -> p (u d)", u=U)

    def ids(t, g, n):
        return t[bass.ds(g * GROUP, n * U)].rearrange("(p u) -> p u", u=U)

    PADP = (EG * GROUP - E) // U

    with ExitStack() as ctx:
        def sb(name, shape, dt=F32):
            return ctx.enter_context(nc.sbuf_tensor(name, shape, dt))

        def ps(name, shape):
            return ctx.enter_context(nc.psum_tensor(name, shape, F32))

        def sem(name):
            return ctx.enter_context(nc.semaphore(name))

        zeros = sb("zeros", [P, ZCOLS])
        ident = sb("ident", [P, P])
        earlier = sb("earlier", [P, P])
        spare = sb("spare", [P, 1])
        before = sb("before", [PLAN, PLAN])
        ones = sb("ones", [P, 1])
        dstp = sb("dstp", [EROWS, ECOLS + 1], I32)
        in_order = sb("in_order", [EROWS, ECOLS])
        blk_hi = sb("blk_hi", [EROWS, ECOLS], I32)
        blk_lo = sb("blk_lo", [EROWS, ECOLS], I32)
        hi16 = sb("hi16", [EROWS, ECOLS], BF16)
        lo16 = sb("lo16", [EROWS, ECOLS], BF16)
        count_to = sb("count_to", [EROWS, PLAN + 1], BF16)
        count_i = sb("count_i", [EROWS, PLAN + 1], I32)
        is_hi = sb("is_hi", [EROWS, ECOLS, PLAN], BF16)
        under_lo = sb("under_lo", [EROWS, ECOLS, PLAN + 1], BF16)
        under = sb("under", [PLAN, PLAN + 1])
        limit = sb("limit", [PLAN, PLAN], I32)
        over = sb("over", [PLAN, 2, PLAN])
        worst = sb("worst", [PLAN, 2])
        worst_over = sb("worst_over", [PLAN, 2])
        faults = sb("faults", [P, 2])
        starts_sb = sb("starts_sb", [PLAN, PLAN], I32)
        starts_row = sb("starts_row", [1, PLAN * PLAN], I32)
        general = sb("general", [1, 1], I32)
        eps = sb("eps", [P, 1])
        we1_er = sb("we1_er", [P, H])
        we1_s = sb("we1_s", [P, 2, H])
        we2_sb = sb("we2_sb", [P, D])
        wn1_sb = sb("wn1_sb", [P, H])
        wn2_sb = sb("wn2_sb", [P, D])
        be1_c = sb("be1_c", [P, 1])
        bn1_c = sb("bn1_c", [P, 1])
        be2_b = sb("be2_b", [P, D])
        bn2_b = sb("bn2_b", [P, D])
        src_id = sb("src_id", [P, 2, U], I32)
        dst_id = sb("dst_id", [P, 2, U], I32)
        edge_recv = sb("edge_recv", [P, 2, U, 2 * D])
        sender = sb("sender", [P, 2, U * D])
        edge_recv_t = sb("edge_recv_t", [P, 2, U * P])
        sender_t = sb("sender_t", [P, 2, 2 * P])
        ehid = sb("ehid", [P, 2, U * P])
        rec = sb("rec", [P, 2, U, REC])
        recin = sb("recin", [P, 2, U, REC])
        same = sb("same", [P, 2, P])
        same_earlier = sb("same_earlier", [P, P])
        n_earlier = sb("n_earlier", [P, 2])
        is_later = sb("is_later", [P, 2])
        to_spare = sb("to_spare", [P, 2])
        row_id = sb("row_id", [P, 2], I32)
        summed = sb("summed", [P, 2, D])
        windows = sb("windows", [P, 2, BLOCKS, REC])
        place = sb("place", [P, P])
        place_i = sb("place_i", [P, P], I32)
        half_base = sb("half_base", [P, BLOCKS])
        half_base_i = sb("half_base_i", [P, BLOCKS], I32)
        in_block = sb("in_block", [P, BLOCKS])
        onehot = sb("onehot", [P, 2, U, P])
        no_message = sb("no_message", [PADP, U, REC])
        xt = sb("xt", [P, 4, (U + 1) * D])
        aggt = sb("aggt", [P, 2, U * D])
        node_t = sb("node_t", [P, 2, U * P])
        nhid = sb("nhid", [P, 2, U * P])
        y = sb("y", [P, 2, U, D])
        stats = sb("stats", [P, 2, U, 6])
        meanvar = sb("meanvar", [P, 2, U, 2])
        std = sb("std", [P, 2, U])
        rstd = sb("rstd", [P, 2, U])
        res = sb("res", [P, 4, U, D])

        ps_er = ps("ps_er", [P, U * P])
        ps_s = ps("ps_s", [P, 512])
        ps_eh = ps("ps_eh", [P, U * P])
        ps_msg = ps("ps_msg", [P, 512])
        ps_node = ps("ps_node", [P, U * P])
        ps_nh2 = [ps(f"ps_nh{i}", [P, U * P]) for i in range(2)]
        ps_new = ps("ps_new", [P, 512])
        ps_ids = ps_s[:, 0:P]
        ps_sum = ps_msg[:, 0:D]
        ps_under = ps_s[0:PLAN, 0:PLAN + 1]
        ps_starts = ps_msg[0:PLAN, 0:PLAN]
        ps_faults = ps_new[0:1, 0:1]

        s_weights = sem("s_weights")
        s_const = sem("s_const")
        s_const2 = sem("s_const2")
        s_halves = sem("s_halves")
        s_zeroed = sem("s_zeroed")
        plan_edge = sem("plan_edge")
        plan_in = sem("plan_in")
        plan_step = sem("plan_step")
        plan_iota = sem("plan_iota")
        plan_onehots = sem("plan_onehots")
        plan_counted = sem("plan_counted")
        plan_under = sem("plan_under")
        plan_summed = sem("plan_summed")
        starts_made = sem("starts_made")
        starts_out = sem("starts_out")
        starts_in = sem("starts_in")
        faults_made = sem("faults_made")
        faults_summed = sem("faults_summed")
        plan_ready = sem("plan_ready")
        pad_made = sem("pad_made")
        pad_out = sem("pad_out")
        windows_in = [sem(f"windows_in{i}") for i in range(2)]
        placed = sem("placed")
        base_moved = sem("base_moved")
        onehot_made = sem("onehot_made")
        ids_in = [sem(f"ids_in{i}") for i in range(2)]
        edges_in = [sem(f"edges_in{i}") for i in range(2)]
        gathered = [sem(f"gathered{i}") for i in range(2)]
        rec_out = [sem(f"rec_out{i}") for i in range(2)]
        dst_noted = sem("dst_noted")
        e_turned = sem("e_turned")
        er_copied = sem("er_copied")
        s_copied = sem("s_copied")
        e_hidden = sem("e_hidden")
        e_relu = sem("e_relu")
        e_msg = sem("e_msg")
        rec_made = sem("rec_made")
        rec_in = [sem(f"rec_in{i}") for i in range(2)]
        ids_spread = sem("ids_spread")
        same_made = sem("same_made")
        counted = sem("counted")
        later_made = sem("later_made")
        spare_made = sem("spare_made")
        row_made = sem("row_made")
        sum_made = sem("sum_made")
        sum_copied = sem("sum_copied")
        scattered = sem("scattered")
        pool_passed = sem("pool_passed")
        dve_passed = sem("dve_passed")
        x_in = [sem(f"x_in{i}") for i in range(2)]
        res_out = [sem(f"res_out{i}") for i in range(2)]
        n_turned = sem("n_turned")
        node_copied = sem("node_copied")
        n_hidden = sem("n_hidden")
        n_relu = sem("n_relu")
        n_new = sem("n_new")
        n_added = sem("n_added")
        n_biased = sem("n_biased")
        n_stats = sem("n_stats")
        n_aggr = sem("n_aggr")
        n_std = sem("n_std")
        n_rstd = sem("n_rstd")
        n_normed = sem("n_normed")

        NWEIGHTS = 10
        block = ctx.enter_context(nc.Block())

        def pairs(eng, begin, end, step):
            step(begin)
            with eng.Fori(begin + 1, end - 1) as i:
                step(i)
            step(end - 1)

        def is_first(i):
            return isinstance(i, int) and i == 0

        def eparts(i, s):
            return ETAIL if isinstance(i, int) and 2 * i + s == EG - 1 else P

        def nparts(q, last):
            return NTAIL if last and isinstance(q, int) and q == NG - 1 else P

        def cols(t, n):
            return t.rearrange("p (u r) -> p u r", u=U)[:, :, 0:n]

        def choose(eng, fast, general_path):
            eng.wait_ge(plan_ready, 1)
            faulty = eng.value_load(general[0:1, 0:1], min_val=0, max_val=1)
            with eng.If(faulty == 0):
                fast()
            with eng.Else():
                general_path()

        def fast_pairs(eng, step, ahead=0):
            step(2)
            with eng.Fori(3, EPAIRS - 1 - ahead) as i:
                step(i)
            for i in range(EPAIRS - 1 - ahead, EPAIRS + 2):
                step(i)

        def has_edges(i):
            return not isinstance(i, int) or i < EPAIRS

        def starts_nodes(i, s):
            return isinstance(i, int) and 2 * i + s == LAG

        def last_half(i, s):
            return isinstance(i, int) and 2 * i + s - LAG == NPAIRS - 1

        @block.sync
        def _(sp):
            for w, a in ((we1_er[:, :], we1[0:2 * D, :]), (we1_s[0:D, 0, :], we1[2 * D:3 * D, :]),
                         (we1_s[D:2 * D, 1, :], we1[2 * D:3 * D, :]), (we2_sb[:, :], we2), (wn1_sb[:, :], wn1),
                         (wn2_sb[:, :], wn2), (be1_c[:, :], be1.rearrange("(h o) -> h o", o=1)),
                         (bn1_c[:, :], bn1.rearrange("(h o) -> h o", o=1)),
                         (be2_b[:, :], be2.rearrange("(a d) -> a d", a=1).to_broadcast([P, D])),
                         (bn2_b[:, :], bn2.rearrange("(a d) -> a d", a=1).to_broadcast([P, D]))):
                sp.dma_start(w, a).then_inc(s_weights, 16)

            def load_edges(i, s):
                g = 2 * i + s
                n = eparts(i, s)
                if not is_first(i):
                    sp.wait_ge(gathered[s], 2 * U * 16 * i)
                    sp.wait_ge(dst_noted, g - 1)
                sp.dma_start(src_id[0:n, s, :], ids(src, g, n)).then_inc(ids_in[s], 16)
                sp.dma_start(dst_id[0:n, s, :], ids(dst, g, n)).then_inc(ids_in[s], 16)
                if not is_first(i):
                    sp.wait_ge(e_turned, g - 1)
                sp.dma_start(edge_recv[0:n, s, :, 0:D],
                             edges[bass.ds(g * GROUP, n * U), :].rearrange("(p u) d -> p u d", u=U))\
                  .then_inc(edges_in[s], 16)

            def store_rec(i, s):
                g = 2 * i + s
                n = eparts(i, s)
                sp.wait_ge(rec_made, g + 1)
                sp.dma_start(rows(messages, g, n, REC), rec[0:n, s, :, :].rearrange("p u d -> p (u d)"))\
                  .then_inc(rec_out[s], 16)

            load_edges(0, 0)
            load_edges(0, 1)
            sp.dma_start(dstp[:, 0:ECOLS], dst.rearrange("(p e) -> p e", e=ECOLS)).then_inc(plan_in, 16)
            sp.wait_ge(plan_edge, 1)
            with nc.allow_non_contiguous_dma(reason="one id of each row"):
                sp.dma_start(dstp[0:EROWS - 1, ECOLS:ECOLS + 1],
                             dst.rearrange("(p e) -> p e", e=ECOLS)[1:EROWS, 0:1]).then_inc(plan_in, 16)
            sp.wait_ge(pad_made, 1)
            sp.dma_start(messages[E:EG * GROUP, :].rearrange("(p u) d -> p u d", u=U), no_message[:, :, :])\
              .then_inc(pad_out, 16)
            for i in range(2):
                for s in range(2):
                    store_rec(i, s)
                    load_edges(i + 1, s)
            sp.wait_ge(starts_made, 1)
            sp.dma_start(starts, starts_sb[:, :]).then_inc(starts_out, 16)
            sp.wait_ge(starts_out, 16)
            sp.dma_start(starts_row[:, :], starts.rearrange("h l -> (h l)").rearrange("(a n) -> a n", a=1))\
              .then_inc(starts_in, 16)

            def fast():
                sp.wait_ge(starts_in, 16)
                sp.wait_ge(pad_out, 16)

                def load_half(h, slot, use, reused):
                    if reused:
                        sp.wait_ge(n_turned, 2 * h - 2)
                    for k in range(BLOCKS):
                        start = sp.value_load(starts_row[0:1, bass.ds(h * BLOCKS + k, 1)], min_val=0, max_val=E)
                        sp.dma_start(windows[:, slot, k, :], messages[bass.ds(start, BLOCK_EDGES), :])\
                          .then_inc(windows_in[slot], 16)
                    if reused:
                        sp.wait_ge(n_added, 2 * h - 2)
                    if isinstance(h, int) and h == NPAIRS - 1:
                        for w, n in ((0, P), (1, NTAIL)):
                            sp.dma_start(xt[0:n, 2 * slot + w, D:(U + 1) * D], rows(x, 2 * h + w, n, D))\
                              .then_inc(x_in[slot], 16)
                    else:
                        sp.dma_start(xt[:, 2 * slot:2 * slot + 2, D:(U + 1) * D],
                                     x[bass.ds(h * HALF, HALF), :].rearrange("(w p u) d -> p w (u d)", w=2, u=U))\
                          .then_inc(x_in[slot], 16)

                def store_half(h, slot):
                    sp.wait_ge(n_normed, 2 * h + 2)
                    if isinstance(h, int) and h == NPAIRS - 1:
                        for w, n in ((0, P), (1, NTAIL)):
                            sp.dma_start(rows(out, 2 * h + w, n, D),
                                         res[0:n, 2 * slot + w, :, :].rearrange("p u d -> p (u d)"))\
                              .then_inc(res_out[slot], 16)
                    else:
                        sp.dma_start(out[bass.ds(h * HALF, HALF), :].rearrange("(w p u) d -> p w (u d)", w=2, u=U),
                                     res[:, 2 * slot:2 * slot + 2, :, :].rearrange("p w u d -> p w (u d)"))\
                          .then_inc(res_out[slot], 16)

                sp.wait_ge(rec_out[0], 32)
                sp.wait_ge(rec_out[1], 16)
                load_half(0, 0, 0, False)

                def step(i):
                    for s in range(2):
                        g = 2 * i + s
                        if has_edges(i):
                            sp.wait_ge(rec_out[1 - s], 16 * (i + s))
                        elif i == EPAIRS and s == 0:
                            sp.wait_ge(rec_out[1], 16 * EPAIRS)
                        if not (isinstance(i, int) and g - LAG + 1 >= NPAIRS):
                            load_half(g - LAG + 1, 1 - s, None, not starts_nodes(i, s))
                        if not starts_nodes(i, s):
                            store_half(g - LAG - 1, 1 - s)
                        if has_edges(i):
                            store_rec(i, s)
                            if has_edges(i + 1):
                                load_edges(i + 1, s)

                fast_pairs(sp, step, ahead=1)
                store_half(NPAIRS - 1, 1)
                sp.wait_ge(res_out[0], 16 * (NPAIRS // 2))
                sp.wait_ge(res_out[1], 16 * (NPAIRS // 2) + 16)

            def general_path():
                for z in range(ZPARTS):
                    sp.dma_start(sums_flat[:, z, :], zeros[:, :]).then_inc(s_zeroed, 16)
                with sp.Fori(2, EPAIRS - 2) as i:
                    for s in range(2):
                        store_rec(i, s)
                        load_edges(i + 1, s)
                for s in range(2):
                    store_rec(EPAIRS - 2, s)
                    load_edges(EPAIRS - 1, s)
                for s in range(2):
                    store_rec(EPAIRS - 1, s)
                for s in range(2):
                    sp.wait_ge(rec_out[s], 16 * EPAIRS)

                def load_rec(i):
                    for s in range(2):
                        g = 2 * i + s
                        n = eparts(i, s)
                        if not is_first(i):
                            sp.wait_ge(sum_made, U * (g - 1))
                            sp.wait_ge(row_made, U * (g - 1))
                        sp.dma_start(recin[0:n, s, :, :].rearrange("p u d -> p (u d)"), rows(messages, g, n, REC))\
                          .then_inc(rec_in[s], 16)

                pairs(sp, 0, EPAIRS, load_rec)
                sp.wait_ge(scattered, 16 * U * EG)

                def load_nodes(i, s):
                    q = 2 * i + s
                    n = nparts(q, True)
                    if not is_first(i):
                        sp.wait_ge(n_turned, q - 1)
                        sp.wait_ge(n_added, q - 1)
                    sp.dma_start(xt[0:n, s, D:(U + 1) * D], rows(x, q, n, D)).then_inc(x_in[s], 16)
                    sp.dma_start(aggt[0:n, s, :], rows(sums, q, n, D)).then_inc(x_in[s], 16)

                def store_nodes(i, s):
                    q = 2 * i + s
                    n = nparts(q, True)
                    sp.wait_ge(n_normed, q + 1)
                    sp.dma_start(rows(out, q, n, D), res[0:n, s, :, :].rearrange("p u d -> p (u d)"))\
                      .then_inc(res_out[s], 16)

                for s in range(2):
                    load_nodes(0, s)
                with sp.Fori(0, NPAIRS - 2) as i:
                    for s in range(2):
                        load_nodes(i + 1, s)
                        store_nodes(i, s)
                for s in range(2):
                    load_nodes(NPAIRS - 1, s)
                    store_nodes(NPAIRS - 2, s)
                for s in range(2):
                    store_nodes(NPAIRS - 1, s)
                for s in range(2):
                    sp.wait_ge(res_out[s], 16 * NPAIRS)

            choose(sp, fast, general_path)

        @block.gpsimd
        def _(pool):
            pool.memset(zeros[:, :], 0.0).then_inc(s_const, 1)
            pool.memset(ident[:, :], 0.0).then_inc(s_const, 1)
            pool.memset(earlier[:, :], 1.0).then_inc(s_const, 1)
            pool.memset(eps[:, :], EPS).then_inc(s_const, 1)
            pool.memset(xt[:, :, 0:D], 0.0).then_inc(s_const, 1)
            pool.iota(count_i[:, :], pattern=[[1, PLAN + 1]], base=0, channel_multiplier=0).then_inc(plan_iota, 1)
            pool.iota(limit[:, :], pattern=[[GROUP, PLAN // BLOCKS], [0, BLOCKS]],
                      base=KNOWN_GROUPS * GROUP - BLOCK_EDGES, channel_multiplier=PLAN // BLOCKS * GROUP)\
                .then_inc(plan_iota, 1)
            pool.iota(place_i[:, :], pattern=[[1, U], [U, P // U]], base=0, channel_multiplier=0).then_inc(plan_iota, 1)
            pool.iota(half_base_i[:, :], pattern=[[P, BLOCKS]], base=0, channel_multiplier=0).then_inc(plan_iota, 1)
            pool.iota(row_id[:, 0:1], pattern=[[0, 1]], base=N, channel_multiplier=1).then_inc(plan_iota, 1)
            pool.wait_ge(s_const, 5)
            pool.affine_select(out=ident[:, :], in_=ident[:, :], compare_op=ALU.not_equal, fill=1.0,
                               base=0, pattern=[[-1, P]], channel_multiplier=1).then_inc(s_const2, 1)
            pool.affine_select(out=earlier[:, :], in_=earlier[:, :], compare_op=ALU.is_gt, fill=0.0,
                               base=0, pattern=[[-1, P]], channel_multiplier=1).then_inc(s_const2, 1)
            pool.wait_ge(plan_edge, 2)
            pool.affine_select(out=before[:, :], in_=before[:, :], compare_op=ALU.is_gt, fill=0.0,
                               base=0, pattern=[[1, PLAN]], channel_multiplier=-1).then_inc(s_const2, 1)

            def gather(i):
                for s in range(2):
                    g = 2 * i + s
                    n = eparts(i, s)
                    pool.wait_ge(ids_in[s], 32 * i + 32)
                    if not is_first(i):
                        pool.wait_ge(e_turned, g - 1)
                    pool.sem_inc(pool_passed, 1)
                    for u in range(U):
                        pool.indirect_dma_start(
                            out=edge_recv[0:n, s, u, D:2 * D], out_offset=None, in_=x,
                            in_offset=bass.IndirectOffsetOnAxis(ap=dst_id[0:n, s, u:u + 1], axis=0))\
                            .then_inc(gathered[s], 16)
                        pool.indirect_dma_start(
                            out=sender[0:n, s, u * D:(u + 1) * D], out_offset=None, in_=x,
                            in_offset=bass.IndirectOffsetOnAxis(ap=src_id[0:n, s, u:u + 1], axis=0))\
                            .then_inc(gathered[s], 16)

            gather(0)
            gather(1)

            def fast():
                pairs(pool, 2, EPAIRS, gather)

            def general_path():
                pairs(pool, 2, EPAIRS, gather)
                pool.wait_ge(s_zeroed, 16 * ZPARTS)

                def scatter(i):
                    for s in range(2):
                        n = eparts(i, s)
                        for u in range(U):
                            k = U * (2 * i + s) + u
                            pool.wait_ge(row_made, k + 1)
                            pool.wait_ge(sum_copied, k + 1)
                            if not (is_first(i) and s == 0 and u == 0):
                                pool.wait_ge(scattered, 16 * k)
                            pool.sem_inc(pool_passed, 1)
                            pool.indirect_dma_start(
                                out=sums,
                                out_offset=bass.IndirectOffsetOnAxis(ap=row_id[0:n, u % 2:u % 2 + 1], axis=0),
                                in_=summed[0:n, u % 2, :], in_offset=None, compute_op=ALU.add)\
                                .then_inc(scattered, 16)

                pairs(pool, 0, EPAIRS, scatter)

            choose(pool, fast, general_path)

        @block.tensor
        def _(pe):
            pe.wait_ge(plan_onehots, 2)
            for e in range(ECOLS):
                mm = pe.matmul(ps_under, is_hi[:, e, :], under_lo[:, e, :], start=(e == 0), stop=(e == ECOLS - 1))
            mm.then_inc(plan_counted, 1)
            pe.wait_ge(plan_under, 1)
            pe.wait_ge(s_const2, 3)
            pe.matmul(ps_starts, ident[0:PLAN, 0:PLAN], under[:, 0:PLAN], start=True, stop=False)
            pe.matmul(ps_starts, before[:, :], under[:, PLAN:PLAN + 1].to_broadcast([PLAN, PLAN]),
                      start=False, stop=True).then_inc(plan_summed, 1)
            pe.wait_ge(faults_made, 2)
            for c in range(2):
                mm = pe.matmul(ps_faults, faults[:, c:c + 1], ones[:, :], start=(c == 0), stop=(c == 1))
            mm.then_inc(faults_summed, 1)
            pe.wait_ge(s_halves, 2)
            pe.wait_ge(s_weights, 16 * NWEIGHTS)
            pe.wait_ge(starts_made, 1)

            def turn_edges(i, s):
                g = 2 * i + s
                n = eparts(i, s)
                pe.wait_ge(edges_in[s], 16 * i + 16)
                pe.wait_ge(gathered[s], 2 * U * 16 * (i + 1))
                if not (is_first(i) and s == 0):
                    pe.wait_ge(er_copied, g)
                    pe.wait_ge(s_copied, g)
                for u in range(U):
                    pe.transpose(ps_er[:, u * P:u * P + n], edge_recv[0:n, s, u, :], ident[0:n, 0:n])
                for v in range(2):
                    t = pe.transpose(ps_s[:, v * P:v * P + n], sender[0:n, s, v * P:(v + 1) * P], ident[0:n, 0:n])
                t.then_inc(e_turned, 1)

            def hide_edges(i, s):
                g = 2 * i + s
                n = eparts(i, s)
                pe.wait_ge(er_copied, g + 1)
                pe.wait_ge(s_copied, g + 1)
                if not (is_first(i) and s == 0):
                    pe.wait_ge(e_relu, g)
                pe.matmul(cols(ps_eh[:, :], n), we1_er[:, :], cols(edge_recv_t[:, s, :], n), start=True, stop=False)
                for h in range(2):
                    mm = pe.matmul(ps_eh[:, :].rearrange("p (v h r) -> p h v r", v=2, h=2)[:, h, :, 0:n],
                                   we1_s[:, h, :],
                                   sender_t[:, s, :].rearrange("p (v r) -> p v r", v=2)[:, :, 0:n],
                                   start=False, stop=(h == 1))
                mm.then_inc(e_hidden, 1)

            def message_edges(i, s):
                g = 2 * i + s
                n = eparts(i, s)
                pe.wait_ge(e_relu, g + 1)
                if not (is_first(i) and s == 0):
                    pe.wait_ge(rec_made, g)
                for u in range(U):
                    mm = pe.matmul(ps_msg[0:n, u * D:(u + 1) * D], ehid[:, s, u * P:u * P + n], we2_sb[:, :],
                                   start=True, stop=True)
                mm.then_inc(e_msg, 1)

            def edge_group(i):
                for s in range(2):
                    turn_edges(i, s)
                    hide_edges(i, s)
                    message_edges(i, s)

            def turn_x(q, w, slot, n, first):
                if not first:
                    pe.wait_ge(node_copied, q)
                for u in range(U):
                    pe.transpose(ps_node[:, u * P:u * P + n], xt[0:n, slot, u * D:(u + 2) * D], ident[0:n, 0:n])

            def hide_nodes(q, w, n, first2):
                pe.wait_ge(node_copied, q + 1)
                if not first2:
                    pe.wait_ge(n_relu, q - 1)
                pe.matmul(cols(ps_nh2[w][:, :], n), wn1_sb[:, :], cols(node_t[:, w, :], n), start=True, stop=True)\
                  .then_inc(n_hidden, 1)

            def new_nodes(q, w, n, first):
                pe.wait_ge(n_relu, q + 1)
                if not first:
                    pe.wait_ge(n_added, q)
                for u in range(U):
                    mm = pe.matmul(ps_new[0:n, u * D:(u + 1) * D],
                                   nhid[:, w, u * P:u * P + n], wn2_sb[:, :], start=True, stop=True)
                mm.then_inc(n_new, 1)

            edge_group(0)
            edge_group(1)

            def fast():
                def turn_nodes(i, s, w):
                    h = 2 * i + s - LAG
                    q = 2 * h + w
                    if w == 0:
                        pe.wait_ge(windows_in[s], 16 * BLOCKS * (i - 1))
                        x_parts = 2 if last_half(i, s) else 1
                        pe.wait_ge(x_in[s], 16 * (i - 2 + x_parts))
                    turn_x(q, w, 2 * s + w, nparts(q, True), starts_nodes(i, s) and w == 0)
                    pe.wait_ge(onehot_made, q + 1)
                    for b in range(U):
                        mm = pe.matmul(ps_node[0:D, :].rearrange("p (u b r) -> p b u r", u=U, b=U)[:, b, :, :],
                                       windows[:, s, U * w + b, 0:D],
                                       onehot[:, w, b, :].rearrange("p (u r) -> p u r", u=U), start=True, stop=True)
                    mm.then_inc(n_turned, 1)

                def step(i):
                    for s in range(2):
                        q = 2 * (2 * i + s - LAG)
                        first = starts_nodes(i, s)
                        if has_edges(i):
                            turn_edges(i, s)
                        if not first:
                            new_nodes(q - 1, 1, P, False)
                        turn_nodes(i, s, 0)
                        if has_edges(i):
                            hide_edges(i, s)
                        turn_nodes(i, s, 1)
                        hide_nodes(q, 0, P, first)
                        if has_edges(i):
                            message_edges(i, s)
                        hide_nodes(q + 1, 1, nparts(q + 1, True), first)
                        new_nodes(q, 0, P, first)

                fast_pairs(pe, step)
                new_nodes(NG - 1, 1, NTAIL, False)

            def general_path():
                pairs(pe, 2, EPAIRS, edge_group)

                def sum_group(i):
                    for s in range(2):
                        n = eparts(i, s)
                        pe.wait_ge(rec_in[s], 16 * i + 16)
                        for u in range(U):
                            k = U * (2 * i + s) + u
                            began = not (is_first(i) and s == 0 and u == 0)
                            if began:
                                pe.wait_ge(same_made, k)
                            pe.matmul(ps_ids[:, 0:n], recin[0:n, s, u, D:D + 1].to_broadcast([n, P]),
                                      ident[0:n, 0:n], start=True, stop=True).then_inc(ids_spread, 1)
                            pe.wait_ge(same_made, k + 1)
                            if began:
                                pe.wait_ge(sum_copied, k)
                            pe.matmul(ps_sum[0:n, :], same[0:n, u % 2, 0:n], recin[0:n, s, u, 0:D],
                                      start=True, stop=True).then_inc(sum_made, 1)

                pairs(pe, 0, EPAIRS, sum_group)

                def node_group(i):
                    for s in range(2):
                        q = 2 * i + s
                        n = nparts(q, True)
                        pe.wait_ge(x_in[s], 32 * i + 32)
                        turn_x(q, s, s, n, is_first(i) and s == 0)
                        for u in range(U):
                            t = pe.transpose(ps_node[0:D, u * P:u * P + n], aggt[0:n, s, u * D:(u + 1) * D],
                                             ident[0:n, 0:n])
                        t.then_inc(n_turned, 1)
                        hide_nodes(q, s, n, is_first(i))
                        new_nodes(q, s, n, is_first(i) and s == 0)

                pairs(pe, 0, NPAIRS, node_group)

            choose(pe, fast, general_path)

        @block.scalar
        def _(act):
            act.wait_ge(s_weights, 16 * NWEIGHTS)
            act.wait_ge(s_const, 5)

            def copy_senders(i, s):
                g = 2 * i + s
                n = eparts(i, s)
                act.wait_ge(e_turned, g + 1)
                if not is_first(i):
                    act.wait_ge(e_hidden, g - 1)
                act.activation(sender_t[:, s, :].rearrange("p (v r) -> p v r", v=2)[:, :, 0:n],
                               ps_s[:, 0:2 * P].rearrange("p (v r) -> p v r", v=2)[:, :, 0:n], ACT.Copy)\
                   .then_inc(s_copied, 1)

            def relu_edges(i, s):
                g = 2 * i + s
                n = eparts(i, s)
                act.wait_ge(e_hidden, g + 1)
                if not is_first(i):
                    act.wait_ge(e_msg, g - 1)
                act.activation(cols(ehid[:, s, :], n), cols(ps_eh[:, :], n), ACT.Relu, bias=be1_c[:, 0:1])\
                   .then_inc(e_relu, 1)

            def edge_group(i):
                for s in range(2):
                    copy_senders(i, s)
                    relu_edges(i, s)

            def copy_nodes(q, w, n, first2):
                act.wait_ge(n_turned, q + 1)
                if not first2:
                    act.wait_ge(n_hidden, q - 1)
                act.activation(cols(node_t[:, w, :], n), cols(ps_node[:, :], n), ACT.Copy).then_inc(node_copied, 1)

            def relu_nodes(q, w, n, first2):
                act.wait_ge(n_hidden, q + 1)
                if not first2:
                    act.wait_ge(n_new, q - 1)
                act.activation(cols(nhid[:, w, :], n), cols(ps_nh2[w][:, :], n), ACT.Relu, bias=bn1_c[:, 0:1])\
                   .then_inc(n_relu, 1)

            def root_nodes(q, w, n, first2):
                act.wait_ge(n_aggr, q + 1)
                if not first2:
                    act.wait_ge(n_rstd, q - 1)
                act.activation(std[0:n, w, :], meanvar[0:n, w, :, 1], ACT.Sqrt, bias=eps[0:n, 0:1])\
                   .then_inc(n_std, 1)

            edge_group(0)
            edge_group(1)

            def fast():
                def step(i):
                    for s in range(2):
                        q = 2 * (2 * i + s - LAG)
                        first = starts_nodes(i, s)
                        second = starts_nodes(i, s - 1)
                        if has_edges(i):
                            copy_senders(i, s)
                        if not first:
                            root_nodes(q - 2, 0, P, second)
                        copy_nodes(q, 0, P, first)
                        if not first:
                            root_nodes(q - 1, 1, P, second)
                        if has_edges(i):
                            relu_edges(i, s)
                        copy_nodes(q + 1, 1, nparts(q + 1, True), first)
                        relu_nodes(q, 0, P, first)
                        relu_nodes(q + 1, 1, nparts(q + 1, True), first)

                fast_pairs(act, step)
                root_nodes(NG - 2, 0, P, False)
                root_nodes(NG - 1, 1, NTAIL, False)

            def general_path():
                pairs(act, 2, EPAIRS, edge_group)

                def sum_group(i):
                    for s in range(2):
                        n = eparts(i, s)
                        for u in range(U):
                            k = U * (2 * i + s) + u
                            act.wait_ge(sum_made, k + 1)
                            if not (is_first(i) and s == 0 and u < 2):
                                act.wait_ge(scattered, 16 * (k - 1))
                            act.activation(summed[0:n, u % 2, :], ps_sum[0:n, :], ACT.Copy).then_inc(sum_copied, 1)

                pairs(act, 0, EPAIRS, sum_group)

                def node_group(i):
                    for s in range(2):
                        q = 2 * i + s
                        n = nparts(q, True)
                        copy_nodes(q, s, n, is_first(i))
                        relu_nodes(q, s, n, is_first(i))
                        root_nodes(q, s, n, is_first(i))

                pairs(act, 0, NPAIRS, node_group)

            choose(act, fast, general_path)

        @block.vector
        def _(dve):
            dve.memset(dstp[:, ECOLS:ECOLS + 1], PLAN * PLAN * P).then_inc(plan_edge, 1)
            dve.memset(before[:, :], 1.0).then_inc(plan_edge, 1)
            dve.memset(we1_s[D:2 * D, 0, :], 0.0).then_inc(s_halves, 1)
            dve.memset(we1_s[0:D, 1, :], 0.0).then_inc(s_halves, 1)
            dve.memset(no_message[:, :, :], 0.0).then_inc(plan_step, 1)
            dve.memset(faults[:, :], 0.0).then_inc(plan_step, 1)
            dve.memset(ones[:, :], 1.0).then_inc(plan_step, 1)
            dve.wait_ge(plan_step, 3)
            dve.memset(no_message[:, :, D:REC], -1.0).then_inc(pad_made, 1)
            dve.wait_ge(plan_iota, 5)
            dve.tensor_copy(count_to[:, :], count_i[:, :]).then_inc(plan_step, 1)
            dve.tensor_copy(place[:, :], place_i[:, :]).then_inc(placed, 1)
            dve.tensor_copy(half_base[:, :], half_base_i[:, :]).then_inc(base_moved, 1)
            dve.tensor_copy(spare[:, :], row_id[:, 0:1]).then_inc(placed, 1)
            dve.wait_ge(plan_in, 32)
            dve.tensor_scalar(blk_hi[:, :], dstp[:, 0:ECOLS], (P * PLAN).bit_length() - 1, None,
                              ALU.arith_shift_right).then_inc(plan_step, 1)
            dve.tensor_scalar(blk_lo[:, :], dstp[:, 0:ECOLS], P.bit_length() - 1, PLAN - 1,
                              ALU.arith_shift_right, ALU.bitwise_and).then_inc(plan_step, 1)
            dve.tensor_tensor(in_order[:, :], dstp[:, 0:ECOLS], dstp[:, 1:ECOLS + 1], ALU.is_gt)\
               .then_inc(plan_step, 1)
            dve.wait_ge(plan_step, 7)
            dve.tensor_copy(hi16[:, :], blk_hi[:, :]).then_inc(plan_step, 1)
            dve.tensor_copy(lo16[:, :], blk_lo[:, :]).then_inc(plan_step, 1)
            dve.tensor_reduce(faults[0:EROWS, 0:1], in_order[:, :], AX_X, ALU.max).then_inc(faults_made, 1)
            dve.wait_ge(plan_step, 9)
            dve.tensor_tensor(is_hi[:, :, :], hi16[:, :].unsqueeze(2).to_broadcast([EROWS, ECOLS, PLAN]),
                              count_to[:, 0:PLAN].unsqueeze(1).to_broadcast([EROWS, ECOLS, PLAN]), ALU.is_equal)\
               .then_inc(plan_onehots, 1)
            dve.tensor_tensor(under_lo[:, :, :], lo16[:, :].unsqueeze(2).to_broadcast([EROWS, ECOLS, PLAN + 1]),
                              count_to[:, :].unsqueeze(1).to_broadcast([EROWS, ECOLS, PLAN + 1]), ALU.is_lt)\
               .then_inc(plan_onehots, 1)
            dve.wait_ge(plan_counted, 1)
            dve.tensor_copy(under[:, :], ps_under).then_inc(plan_under, 1)
            dve.wait_ge(plan_under, 1)
            dve.tensor_tensor(over[:, 0, :], under[:, 1:PLAN + 1], under[:, 0:PLAN], ALU.subtract).then_inc(plan_step, 1)
            dve.wait_ge(plan_summed, 1)
            dve.tensor_copy(starts_sb[:, :], ps_starts).then_inc(starts_made, 1)
            dve.tensor_tensor(over[:, 1, :], ps_starts, limit[:, :], ALU.subtract).then_inc(plan_step, 1)
            dve.wait_ge(plan_step, 11)
            dve.tensor_reduce(worst[:, :], over[:, :, :], AX_X, ALU.max).then_inc(plan_step, 1)
            dve.wait_ge(plan_step, 12)
            dve.tensor_scalar(worst_over[:, 0:1], worst[:, 0:1], float(BLOCK_EDGES), None, ALU.is_gt)\
               .then_inc(plan_step, 1)
            dve.tensor_scalar(worst_over[:, 1:2], worst[:, 1:2], 0.0, None, ALU.is_gt).then_inc(plan_step, 1)
            dve.wait_ge(plan_step, 14)
            dve.tensor_tensor(faults[0:PLAN, 1:2], worst_over[:, 0:1], worst_over[:, 1:2], ALU.max)\
               .then_inc(faults_made, 1)
            dve.wait_ge(faults_summed, 1)
            dve.tensor_scalar(general[:, :], ps_faults, 1.0, None, ALU.min).then_inc(plan_ready, 1)
            dve.wait_ge(s_weights, 16 * NWEIGHTS)

            def note_receivers(i, s):
                g = 2 * i + s
                n = eparts(i, s)
                dve.wait_ge(ids_in[s], 32 * i + 32)
                if not is_first(i):
                    dve.wait_ge(rec_out[s], 16 * i)
                dve.tensor_copy(rec[0:n, s, :, D:D + 2], dst_id[0:n, s, :].unsqueeze(2).to_broadcast([n, U, 2]))\
                   .then_inc(dst_noted, 1)

            def copy_edges(i, s):
                g = 2 * i + s
                n = eparts(i, s)
                dve.wait_ge(e_turned, g + 1)
                if not is_first(i):
                    dve.wait_ge(e_hidden, g - 1)
                dve.tensor_copy(cols(edge_recv_t[:, s, :], n), cols(ps_er[:, :], n)).then_inc(er_copied, 1)

            def make_rec(i, s):
                g = 2 * i + s
                n = eparts(i, s)
                dve.wait_ge(e_msg, g + 1)
                dve.tensor_tensor(rec[0:n, s, :, 0:D], ps_msg[0:n, 0:U * D].rearrange("p (u d) -> p u d", u=U),
                                  be2_b[0:n, :].unsqueeze(1).to_broadcast([n, U, D]), ALU.add)\
                   .then_inc(rec_made, 1)

            def edge_group(i):
                for s in range(2):
                    note_receivers(i, s)
                    copy_edges(i, s)
                    make_rec(i, s)

            def add_nodes(q, w, slot, n, first2):
                dve.wait_ge(n_new, q + 1)
                if not first2:
                    dve.wait_ge(n_normed, q - 1)
                dve.tensor_tensor(y[0:n, w, :, :].rearrange("p u d -> p (u d)"),
                                  ps_new[0:n, 0:U * D],
                                  xt[0:n, slot, D:(U + 1) * D], ALU.add).then_inc(n_added, 1)
                dve.wait_ge(n_added, q + 1)
                dve.tensor_tensor(y[0:n, w, :, :], y[0:n, w, :, :],
                                  bn2_b[0:n, :].unsqueeze(1).to_broadcast([n, U, D]), ALU.add).then_inc(n_biased, 1)
                dve.wait_ge(n_biased, q + 1)
                for u in range(U):
                    st = dve.bn_stats(stats[0:n, w, u, :], y[0:n, w, u, :])
                st.then_inc(n_stats, 1)
                dve.wait_ge(n_stats, q + 1)
                if not first2:
                    dve.wait_ge(n_std, q - 1)
                dve.sem_inc(dve_passed, 1)
                for u in range(U):
                    ag = dve.bn_aggr(meanvar[0:n, w, u, :], stats[0:n, w, u, :])
                ag.then_inc(n_aggr, 1)

            def norm_nodes(q, w, slot, n):
                dve.wait_ge(n_std, q + 1)
                dve.reciprocal(rstd[0:n, w, :], std[0:n, w, :]).then_inc(n_rstd, 1)
                dve.wait_ge(n_rstd, q + 1)
                for u in range(U):
                    nm = dve.tensor_scalar(res[0:n, slot, u, :], y[0:n, w, u, :], meanvar[0:n, w, u, 0:1],
                                           rstd[0:n, w, u:u + 1], ALU.subtract, ALU.mult)
                nm.then_inc(n_normed, 1)

            edge_group(0)
            edge_group(1)

            def fast():
                def make_onehots(h, slot, use, first):
                    dve.wait_ge(windows_in[slot], 16 * BLOCKS * (use + 1))
                    if not first:
                        dve.wait_ge(onehot_made, 2 * h)
                    dve.wait_ge(base_moved, h + 1)
                    dve.tensor_tensor(in_block[:, :], windows[:, slot, :, D], half_base[:, :], ALU.subtract)\
                       .then_inc(placed, 1)
                    dve.wait_ge(placed, h + 3)
                    dve.tensor_scalar(half_base[:, :], half_base[:, :], float(HALF), None, ALU.add)\
                       .then_inc(base_moved, 1)
                    for w in range(2):
                        if not first:
                            dve.wait_ge(n_turned, 2 * h - 1 + w)
                        for b in range(U):
                            oh = dve.tensor_scalar(onehot[:, w, b, :], place[:, :],
                                                   in_block[:, U * w + b:U * w + b + 1], None, ALU.is_equal)
                        oh.then_inc(onehot_made, 1)

                def finish(q, s, use, n_b, second):
                    if not (isinstance(use, int) and use == 0):
                        dve.wait_ge(res_out[s], 16 * use)
                    norm_nodes(q, 0, 2 * s, P)
                    add_nodes(q + 1, 1, 2 * s + 1, n_b, second)
                    norm_nodes(q + 1, 1, 2 * s + 1, n_b)

                dve.wait_ge(placed, 2)
                make_onehots(0, 0, 0, True)

                def step(i):
                    for s in range(2):
                        h = 2 * i + s - LAG
                        q = 2 * h
                        first = starts_nodes(i, s)
                        if has_edges(i):
                            note_receivers(i, s)
                            copy_edges(i, s)
                        if not first:
                            finish(q - 2, 1 - s, i - 3 + s, P, starts_nodes(i, s - 1))
                        if has_edges(i):
                            make_rec(i, s)
                        if not (isinstance(i, int) and h + 1 >= NPAIRS):
                            make_onehots(h + 1, 1 - s, i - 2 + s, False)
                        add_nodes(q, 0, 2 * s, P, first)

                fast_pairs(dve, step)
                finish(NG - 2, 1, NPAIRS // 2 - 1, NTAIL, False)

            def general_path():
                pairs(dve, 2, EPAIRS, edge_group)

                def sum_group(i):
                    for s in range(2):
                        n = eparts(i, s)
                        for u in range(U):
                            k = U * (2 * i + s) + u
                            b = u % 2
                            began2 = not (is_first(i) and s == 0 and u < 2)
                            began = not (is_first(i) and s == 0 and u == 0)
                            receiver = recin[0:n, s, u, D:D + 1]
                            if u == 0:
                                dve.wait_ge(rec_in[s], 16 * i + 16)
                            dve.wait_ge(ids_spread, k + 1)
                            if began2:
                                dve.wait_ge(sum_made, k - 1)
                            dve.tensor_scalar(same[0:n, b, 0:n], ps_ids[0:n, 0:n], receiver, None, ALU.is_equal)\
                               .then_inc(same_made, 1)
                            dve.wait_ge(same_made, k + 1)
                            if began:
                                dve.wait_ge(later_made, k)
                            dve.tensor_tensor_reduce(same_earlier[0:n, 0:n], same[0:n, b, 0:n], earlier[0:n, 0:n],
                                                     1.0, 0.0, ALU.mult, ALU.add, n_earlier[0:n, b:b + 1])\
                               .then_inc(counted, 1)
                            dve.wait_ge(counted, k + 1)
                            if began:
                                dve.wait_ge(row_made, k)
                            dve.tensor_scalar(is_later[0:n, b:b + 1], n_earlier[0:n, b:b + 1], 1.0, None, ALU.min)\
                               .then_inc(later_made, 1)
                            dve.tensor_tensor(to_spare[0:n, b:b + 1], spare[0:n, :], receiver, ALU.subtract)\
                               .then_inc(spare_made, 1)
                            dve.wait_ge(later_made, k + 1)
                            dve.wait_ge(spare_made, k + 1)
                            if began2:
                                dve.wait_ge(scattered, 16 * (k - 1))
                            dve.scalar_tensor_tensor(out=row_id[0:n, b:b + 1], in0=to_spare[0:n, b:b + 1],
                                                     scalar=is_later[0:n, b:b + 1], in1=receiver,
                                                     op0=ALU.mult, op1=ALU.add).then_inc(row_made, 1)

                dve.wait_ge(placed, 2)
                pairs(dve, 0, EPAIRS, sum_group)

                def node_group(i):
                    for s in range(2):
                        q = 2 * i + s
                        n = nparts(q, True)
                        add_nodes(q, s, s, n, is_first(i))
                        if not is_first(i):
                            dve.wait_ge(res_out[s], 16 * i)
                        norm_nodes(q, s, s, n)

                pairs(dve, 0, NPAIRS, node_group)

            choose(dve, fast, general_path)


_INS = ['x', 'src', 'dst', 'edge_attr_64', 'L0_gnn_We1', 'L0_gnn_be1', 'L0_gnn_We2', 'L0_gnn_be2',
        'L0_gnn_Wn1', 'L0_gnn_bn1', 'L0_gnn_Wn2', 'L0_gnn_bn2']


def kernel(**inputs):
    import numpy as _np
    import concourse.bacc as _bacc
    from concourse import mybir as _mybir
    from concourse.bass_utils import run_bass_kernel_spmd as _run

    nc = _bacc.Bacc("TRN2", target_bir_lowering=False, num_devices=1)
    arrays, args = {}, []
    for name in _INS:
        a = _np.ascontiguousarray(inputs[name])
        arrays[f"in_{name}"] = a
        args.append(nc.dram_tensor(f"in_{name}", a.shape, _mybir.dt.from_np(a.dtype), kind="ExternalInput").ap())
    out = nc.dram_tensor("out_0", inputs['x'].shape, F32, kind="ExternalOutput").ap()
    gnn_resnorm(nc, *args, out)
    r = _run(nc, [arrays], core_ids=[0])
    return r.results[0]["out_0"]
```

```python
from contextlib import ExitStack

import concourse.bass as bass
from concourse import mybir

P = 128
F32 = mybir.dt.float32
F32R = mybir.dt.float32r
BF16 = mybir.dt.bfloat16
AX_X = mybir.AxisListType.X
I32 = mybir.dt.int32
ALU = mybir.AluOpType
ACT = mybir.ActivationFunctionType

U = 4
GROUP = U * P
EPS = 1e-5


def gnn_resnorm(nc, x, src, dst, edges, we1, be1, we2, be2, wn1, bn1, wn2, bn2, out):
    N, D = x.shape
    E = src.shape[0]
    H = we1.shape[1]
    REC = D + 2
    EG = -(-E // GROUP)
    ETAIL = (E - (EG - 1) * GROUP) // U
    NG = -(-N // GROUP)
    NTAIL = (N - (NG - 1) * GROUP) // U
    assert D == 64 and H == P and EG % 2 == 0 and NG % 2 == 0
    assert (EG - 1) * GROUP + ETAIL * U == E and (NG - 1) * GROUP + NTAIL * U == N
    EPAIRS, NPAIRS = EG // 2, NG // 2
    BLOCK_EDGES = P
    HALF = 2 * GROUP
    BLOCKS = HALF // P
    LAG = 5
    KNOWN_GROUPS = LAG - 2
    FIRST_GROUPS = 5
    PLAN = 32
    EROWS = 125
    ECOLS = E // EROWS
    PLAN_PARTS = 4
    assert EROWS * ECOLS == E and N <= PLAN * PLAN * P and NPAIRS == EG and E + P <= EG * GROUP

    starts = nc.dram_tensor("starts", [PLAN, PLAN], I32, kind="Internal").ap()
    messages = nc.dram_tensor("messages", [EG * GROUP, REC], F32, kind="Internal").ap()
    sums = nc.dram_tensor("sums", [N + P, D], F32, kind="Internal").ap()
    ZPARTS = 12
    ZCOLS = (N + P) * D // P // ZPARTS
    assert ZCOLS * P * ZPARTS == (N + P) * D
    sums_flat = sums.rearrange("n d -> (n d)").rearrange("(p z c) -> p z c", p=P, z=ZPARTS)

    def rows(t, g, n, width):
        return t[bass.ds(g * GROUP, n * U), :].rearrange("(p u) d -> p (u d)", u=U)

    PADP = (EG * GROUP - E) // U

    with ExitStack() as ctx:
        def sb(name, shape, dt=F32):
            return ctx.enter_context(nc.sbuf_tensor(name, shape, dt))

        def ps(name, shape):
            return ctx.enter_context(nc.psum_tensor(name, shape, F32))

        def sem(name):
            return ctx.enter_context(nc.semaphore(name))

        zeros = sb("zeros", [P, ZCOLS])
        ident = sb("ident", [P, P])
        earlier = sb("earlier", [P, P])
        spare = sb("spare", [P, 1])
        before = sb("before", [PLAN, PLAN])
        ones = sb("ones", [P, 1])
        dstp = sb("dstp", [EROWS, ECOLS + 1], I32)
        in_order = sb("in_order", [EROWS, ECOLS])
        blk_hi = sb("blk_hi", [EROWS, ECOLS], I32)
        blk_lo = sb("blk_lo", [EROWS, ECOLS], I32)
        hi16 = sb("hi16", [EROWS, ECOLS], BF16)
        lo16 = sb("lo16", [EROWS, ECOLS], BF16)
        count_to = sb("count_to", [EROWS, PLAN + 1], BF16)
        count_i = sb("count_i", [EROWS, PLAN + 1], I32)
        is_hi = sb("is_hi", [EROWS, ECOLS, PLAN], BF16)
        under_lo = sb("under_lo", [EROWS, ECOLS, PLAN + 1], BF16)
        under = sb("under", [PLAN, PLAN + 1])
        limit = sb("limit", [PLAN, PLAN], I32)
        over = sb("over", [PLAN, 2, PLAN])
        worst = sb("worst", [PLAN, 2])
        worst_over = sb("worst_over", [PLAN, 2])
        faults = sb("faults", [P, 2])
        starts_sb = sb("starts_sb", [PLAN, PLAN], I32)
        starts_row = sb("starts_row", [1, PLAN * PLAN], I32)
        general = sb("general", [1, 1], I32)
        eps = sb("eps", [P, 1])
        warm = sb("warm", [P, 1])
        we1_er = sb("we1_er", [P, H])
        we1_s = sb("we1_s", [P, 2, H])
        we2_sb = sb("we2_sb", [P, D])
        wn1_sb = sb("wn1_sb", [P, H])
        wn2_sb = sb("wn2_sb", [P, D])
        be1_c = sb("be1_c", [P, 1])
        bn1_c = sb("bn1_c", [P, 1])
        be2_b = sb("be2_b", [P, D])
        bn2_b = sb("bn2_b", [P, D])
        end_ids = sb("end_ids", [P, EG, 2, U], I32)
        id_rows = sb("id_rows", [EG, 2, GROUP], I32)
        id_rows_f = sb("id_rows_f", [EG, 2, GROUP])
        gather_ids = sb("gather_ids", [P, 2, 2, U], I32)
        edge_recv = sb("edge_recv", [P, 2, U, 2 * D])
        sender = sb("sender", [P, 2, U * D])
        edge_recv_t = sb("edge_recv_t", [P, 2, U * P])
        sender_t = sb("sender_t", [P, 2, 2 * P])
        ehid = sb("ehid", [P, 2, U * P])
        rec = sb("rec", [P, 2, U, REC])
        recin = sb("recin", [P, 2, U, REC])
        same = sb("same", [P, 2, P])
        same_earlier = sb("same_earlier", [P, P])
        n_earlier = sb("n_earlier", [P, 2])
        is_later = sb("is_later", [P, 2])
        to_spare = sb("to_spare", [P, 2])
        row_id = sb("row_id", [P, 2], I32)
        summed = sb("summed", [P, 2, D])
        windows = sb("windows", [P, 2, BLOCKS, REC])
        windows_hi = sb("windows_hi", [P, 2, BLOCKS, D], F32R)
        windows_lo = sb("windows_lo", [P, 2, BLOCKS, D], F32R)
        place = sb("place", [P, P])
        place_i = sb("place_i", [P, P], I32)
        half_base = sb("half_base", [P, BLOCKS])
        half_base_i = sb("half_base_i", [P, BLOCKS], I32)
        in_block = sb("in_block", [P, 2, BLOCKS])
        onehot = sb("onehot", [P, 2, BLOCKS, P], F32R)
        no_message = sb("no_message", [PADP, U, REC])
        xt = sb("xt", [P, 4, (U + 1) * D])
        aggt = sb("aggt", [P, 4, U * D])
        node_t = sb("node_t", [P, 2, U * P])
        nhid = sb("nhid", [P, 2, U * P])
        y = sb("y", [P, 2, U * D])
        stats = sb("stats", [P, 2 * U, 6])
        meanvar = sb("meanvar", [P, 2 * U, 2])
        std = sb("std", [P, 2 * U])
        rstd = sb("rstd", [P, 2 * U])
        res = sb("res", [P, 4, U * D])

        ps_er = ps("ps_er", [P, U * P])
        ps_s = ps("ps_s", [P, 512])
        ps_eh = ps("ps_eh", [P, U * P])
        ps_msg = ps("ps_msg", [P, 512])
        ps_node = ps("ps_node", [P, U * P])
        ps_nh2 = [ps(f"ps_nh{i}", [P, U * P]) for i in range(2)]
        ps_new = ps("ps_new", [P, 512])
        ps_ids = ps_s[:, 0:P]
        ps_sum = ps_msg[:, 0:D]
        ps_ends = (ps_nh2[1], ps_new)
        ps_under = ps_node[0:PLAN, 0:PLAN + 1]
        ps_starts = ps_nh2[0][0:PLAN, 0:PLAN]
        ps_faults = ps_nh2[1][0:1, 0:1]

        s_weights = sem("s_weights")
        s_const = sem("s_const")
        s_const2 = sem("s_const2")
        s_halves = sem("s_halves")
        zeros_made = sem("zeros_made")
        s_zeroed = sem("s_zeroed")
        warmed = sem("warmed")
        plan_edge = sem("plan_edge")
        plan_in = sem("plan_in")
        plan_step = sem("plan_step")
        plan_iota = sem("plan_iota")
        plan_onehots = sem("plan_onehots")
        plan_counted = sem("plan_counted")
        plan_under = sem("plan_under")
        plan_summed = sem("plan_summed")
        starts_made = sem("starts_made")
        starts_out = sem("starts_out")
        starts_in = sem("starts_in")
        faults_made = sem("faults_made")
        faults_summed = sem("faults_summed")
        plan_ready = sem("plan_ready")
        pad_made = sem("pad_made")
        pad_out = sem("pad_out")
        windows_in = [sem(f"windows_in{i}") for i in range(2)]
        placed = sem("placed")
        base_moved = sem("base_moved")
        high_made = sem("high_made")
        low_made = sem("low_made")
        onehot_made = sem("onehot_made")
        ids_padded = sem("ids_padded")
        ids_staged = sem("ids_staged")
        first_ids_in = sem("first_ids_in")
        more_ids_in = sem("more_ids_in")
        ids_moved = sem("ids_moved")
        ids_turned = sem("ids_turned")
        ids_laid = sem("ids_laid")
        edges_in = [sem(f"edges_in{i}") for i in range(2)]
        gathered = [sem(f"gathered{i}") for i in range(2)]
        rec_out = [sem(f"rec_out{i}") for i in range(2)]
        dst_noted = sem("dst_noted")
        e_turned = sem("e_turned")
        er_copied = sem("er_copied")
        s_copied = sem("s_copied")
        e_hidden = sem("e_hidden")
        e_relu = sem("e_relu")
        e_msg = sem("e_msg")
        rec_made = sem("rec_made")
        rec_in = [sem(f"rec_in{i}") for i in range(2)]
        ids_spread = sem("ids_spread")
        same_made = sem("same_made")
        counted = sem("counted")
        later_made = sem("later_made")
        spare_made = sem("spare_made")
        row_made = sem("row_made")
        sum_made = sem("sum_made")
        sum_copied = sem("sum_copied")
        scattered = sem("scattered")
        pool_passed = sem("pool_passed")
        dve_passed = sem("dve_passed")
        x_in = [sem(f"x_in{i}") for i in range(2)]
        res_out = [sem(f"res_out{i}") for i in range(2)]
        n_turned = sem("n_turned")
        node_copied = sem("node_copied")
        n_hidden = sem("n_hidden")
        n_relu = sem("n_relu")
        n_new = sem("n_new")
        n_added = sem("n_added")
        n_biased = sem("n_biased")
        n_stats = sem("n_stats")
        n_aggr = sem("n_aggr")
        n_std = sem("n_std")
        n_rstd = sem("n_rstd")
        sp_passed = sem("sp_passed")
        n_centered = sem("n_centered")
        n_normed = sem("n_normed")

        NWEIGHTS = 10
        block = ctx.enter_context(nc.Block())

        def pairs(eng, begin, end, step):
            step(begin)
            with eng.Fori(begin + 1, end - 1) as i:
                step(i)
            step(end - 1)

        def is_first(i):
            return isinstance(i, int) and i == 0

        def eparts(i, s):
            return ETAIL if isinstance(i, int) and 2 * i + s == EG - 1 else P

        def cols(t, n):
            return t.rearrange("p (u r) -> p u r", u=U)[:, :, 0:n]

        def choose(eng, fast, general_path):
            eng.wait_ge(plan_ready, 1)
            faulty = eng.value_load(general[0:1, 0:1], min_val=0, max_val=1)
            with eng.If(faulty == 0):
                fast()
            with eng.Else():
                general_path()

        FIRST = 2
        LAST = (NPAIRS - 1 + LAG) // 2

        def fast_pairs(eng, step, ahead=0, behind=0):
            for i in range(FIRST, FIRST + 1 + behind):
                step(i)
            with eng.Fori(FIRST + 1 + behind, EPAIRS - 1 - ahead) as i:
                step(i)
            for i in range(EPAIRS - 1 - ahead, LAST + 1):
                step(i)

        def has_edges(i):
            return not isinstance(i, int) or i < EPAIRS

        def has_half(i, s, off=0):
            return not isinstance(i, int) or 0 <= 2 * i + s - LAG + off < NPAIRS

        def half_is(i, s, h):
            return isinstance(i, int) and 2 * i + s - LAG == h

        def is_last(h):
            return isinstance(h, int) and h == NPAIRS - 1

        def rows_of_half(t, h):
            return t[bass.ds(h * HALF, HALF), :].rearrange("(w p u) d -> p w (u d)", w=2, u=U)

        def load_rows_of_half(eng, t, h, tile, slot, s_done):
            if is_last(h):
                for w, n in ((0, P), (1, NTAIL)):
                    eng.dma_start(tile[0:n, 2 * slot + w, :], rows(t, 2 * h + w, n, D)).then_inc(s_done, 16)
            else:
                eng.dma_start(tile[:, 2 * slot:2 * slot + 2, :], rows_of_half(t, h)).then_inc(s_done, 16)

        def store_rec(eng, i, s):
            g = 2 * i + s
            n = eparts(i, s)
            eng.wait_ge(dst_noted, g + 1)
            eng.wait_ge(rec_made, g + 1)
            eng.dma_start(rows(messages, g, n, REC), rec[0:n, s, :, :].rearrange("p u d -> p (u d)"))\
               .then_inc(rec_out[s], 16)

        @block.sync
        def _(sp):
            sp.dma_start(dstp[:, 0:ECOLS], dst.rearrange("(p e) -> p e", e=ECOLS)).then_inc(plan_in, 16)
            sp.wait_ge(plan_edge, 1)
            with nc.allow_non_contiguous_dma(reason="one id of each row"):
                sp.dma_start(dstp[0:EROWS - 1, ECOLS:ECOLS + 1],
                             dst.rearrange("(p e) -> p e", e=ECOLS)[1:EROWS, 0:1]).then_inc(plan_in, 16)
            for w, a in ((we1_er[:, :], we1[0:2 * D, :]), (we1_s[0:D, 0, :], we1[2 * D:3 * D, :]),
                         (we1_s[D:2 * D, 1, :], we1[2 * D:3 * D, :]), (we2_sb[:, :], we2), (wn1_sb[:, :], wn1),
                         (wn2_sb[:, :], wn2), (be1_c[:, :], be1.rearrange("(h o) -> h o", o=1)),
                         (bn1_c[:, :], bn1.rearrange("(h o) -> h o", o=1)),
                         (be2_b[:, :], be2.rearrange("(a d) -> a d", a=1).to_broadcast([P, D])),
                         (bn2_b[:, :], bn2.rearrange("(a d) -> a d", a=1).to_broadcast([P, D]))):
                sp.dma_start(w, a).then_inc(s_weights, 16)

            sp.wait_ge(pad_made, 1)
            sp.dma_start(messages[E:EG * GROUP, :].rearrange("(p u) d -> p u d", u=U), no_message[:, :, :])\
              .then_inc(pad_out, 16)
            for i, s in ((0, 0), (0, 1), (1, 0)):
                store_rec(sp, i, s)
            sp.wait_ge(starts_made, 1)
            sp.dma_start(starts, starts_sb[:, :]).then_inc(starts_out, 16)
            sp.wait_ge(starts_out, 16)
            sp.dma_start(starts_row[:, :], starts.rearrange("h l -> (h l)").rearrange("(a n) -> a n", a=1))\
              .then_inc(starts_in, 16)
            sp.wait_ge(starts_in, 16)
            sp.wait_ge(pad_out, 16)

            def fast():
                def first_edges(h):
                    _, first = nc.values_load_multi_w_load_instructions(
                        starts_row[0:1, bass.ds(h * BLOCKS, BLOCKS)], engines=[mybir.EngineType.SP],
                        min_val=0, max_val=E, skip_runtime_bounds_check_because="they are counts of some of E edges")
                    return first

                def load_windows(h, first, slot, reused):
                    if reused:
                        sp.wait_ge(low_made, h - 1)
                        sp.sem_inc(sp_passed, 1)
                    for k in range(BLOCKS):
                        sp.dma_start(windows[:, slot, k, :], messages[bass.ds(first[k], BLOCK_EDGES), :])\
                          .then_inc(windows_in[slot], 16)

                def load_x(h, slot, reused):
                    if reused:
                        sp.wait_ge(n_added, h - 1)
                    load_rows_of_half(sp, x, h, xt[:, :, D:(U + 1) * D], slot, x_in[slot])

                sp.wait_ge(rec_out[0], 32)
                sp.wait_ge(rec_out[1], 16)
                load_windows(0, first_edges(0), 0, False)
                load_x(0, 0, False)

                def step(i):
                    for s in range(2):
                        h = 2 * i + s - LAG
                        load_next = has_half(i, s, 1) and not half_is(i, s, -1)
                        if load_next:
                            first = first_edges(h + 1)
                        if has_edges(i):
                            sp.wait_ge(rec_out[s], 16 * i)
                            sp.sem_inc(sp_passed, 1)
                        elif i == EPAIRS:
                            sp.wait_ge(rec_out[s], 16 * EPAIRS)
                        if load_next:
                            load_windows(h + 1, first, s, not half_is(i, s, 0))
                            load_x(h + 1, s, not half_is(i, s, 0))

                fast_pairs(sp, step)

            def general_path():
                sp.wait_ge(zeros_made, 1)
                for z in range(ZPARTS):
                    sp.dma_start(sums_flat[:, z, :], zeros[:, :]).then_inc(s_zeroed, 16)
                store_rec(sp, 1, 1)

                def store_recs(i):
                    for s in range(2):
                        store_rec(sp, i, s)

                pairs(sp, 2, EPAIRS, store_recs)
                for s in range(2):
                    sp.wait_ge(rec_out[s], 16 * EPAIRS)

                def load_rec(i):
                    for s in range(2):
                        g = 2 * i + s
                        n = eparts(i, s)
                        if not is_first(i):
                            sp.wait_ge(sum_made, U * (g - 1))
                            sp.wait_ge(row_made, U * (g - 1))
                        sp.dma_start(recin[0:n, s, :, :].rearrange("p u d -> p (u d)"), rows(messages, g, n, REC))\
                          .then_inc(rec_in[s], 16)

                pairs(sp, 0, EPAIRS, load_rec)
                sp.wait_ge(scattered, 16 * U * EG)

                def load_nodes(i, s):
                    h = 2 * i + s
                    if not is_first(i):
                        sp.wait_ge(n_turned, 2 * h - 2)
                        sp.sem_inc(sp_passed, 1)
                        sp.wait_ge(n_added, h - 1)
                    load_rows_of_half(sp, x, h, xt[:, :, D:(U + 1) * D], s, x_in[s])
                    load_rows_of_half(sp, sums, h, aggt, s, x_in[s])

                for s in range(2):
                    load_nodes(0, s)
                with sp.Fori(0, NPAIRS // 2 - 2) as i:
                    for s in range(2):
                        load_nodes(i + 1, s)
                for s in range(2):
                    load_nodes(NPAIRS // 2 - 1, s)

            choose(sp, fast, general_path)

        @block.gpsimd
        def _(pool):
            pool.memset(ident[:, :], 0.0).then_inc(s_const, 1)
            pool.memset(earlier[:, :], 1.0).then_inc(s_const, 1)
            pool.memset(eps[:, :], EPS).then_inc(s_const, 1)
            pool.memset(xt[:, :, 0:D], 0.0).then_inc(s_const, 1)
            pool.iota(count_i[:, :], pattern=[[1, PLAN + 1]], base=0, channel_multiplier=0).then_inc(plan_iota, 1)
            pool.iota(limit[:, :], pattern=[[GROUP, PLAN // BLOCKS], [0, BLOCKS]],
                      base=KNOWN_GROUPS * GROUP - BLOCK_EDGES, channel_multiplier=PLAN // BLOCKS * GROUP)\
                .then_inc(plan_iota, 1)
            pool.iota(place_i[:, :], pattern=[[1, U], [U, P // U]], base=0, channel_multiplier=0).then_inc(plan_iota, 1)
            pool.iota(half_base_i[:, :], pattern=[[P, BLOCKS]], base=0, channel_multiplier=0).then_inc(plan_iota, 1)
            pool.iota(row_id[:, 0:1], pattern=[[0, 1]], base=N, channel_multiplier=1).then_inc(plan_iota, 1)
            pool.wait_ge(s_const, 4)
            pool.affine_select(out=ident[:, :], in_=ident[:, :], compare_op=ALU.not_equal, fill=1.0,
                               base=0, pattern=[[-1, P]], channel_multiplier=1).then_inc(s_const2, 1)
            pool.affine_select(out=earlier[:, :], in_=earlier[:, :], compare_op=ALU.is_gt, fill=0.0,
                               base=0, pattern=[[-1, P]], channel_multiplier=1).then_inc(s_const2, 1)
            pool.wait_ge(plan_edge, 2)
            pool.affine_select(out=before[:, :], in_=before[:, :], compare_op=ALU.is_gt, fill=0.0,
                               base=0, pattern=[[1, PLAN]], channel_multiplier=-1).then_inc(s_const2, 1)

            def gather(i):
                for s in range(2):
                    g = 2 * i + s
                    n = P
                    pool.wait_ge(ids_staged, g + 1)
                    if not is_first(i):
                        pool.wait_ge(e_turned, g - 1)
                    pool.sem_inc(pool_passed, 1)
                    for u in range(U):
                        pool.indirect_dma_start(
                            out=edge_recv[0:n, s, u, D:2 * D], out_offset=None, in_=x,
                            in_offset=bass.IndirectOffsetOnAxis(ap=gather_ids[:, s, 1, u:u + 1], axis=0))\
                            .then_inc(gathered[s], 16)
                        pool.indirect_dma_start(
                            out=sender[0:n, s, u * D:(u + 1) * D], out_offset=None, in_=x,
                            in_offset=bass.IndirectOffsetOnAxis(ap=gather_ids[:, s, 0, u:u + 1], axis=0))\
                            .then_inc(gathered[s], 16)

            pairs(pool, 0, EPAIRS, gather)

            def fast():
                pass

            def general_path():
                pool.wait_ge(s_zeroed, 16 * ZPARTS)

                def scatter(i):
                    for s in range(2):
                        n = eparts(i, s)
                        for u in range(U):
                            k = U * (2 * i + s) + u
                            pool.wait_ge(row_made, k + 1)
                            pool.wait_ge(sum_copied, k + 1)
                            if not (is_first(i) and s == 0 and u == 0):
                                pool.wait_ge(scattered, 16 * k)
                            pool.sem_inc(pool_passed, 1)
                            pool.indirect_dma_start(
                                out=sums,
                                out_offset=bass.IndirectOffsetOnAxis(ap=row_id[0:n, u % 2:u % 2 + 1], axis=0),
                                in_=summed[0:n, u % 2, :], in_offset=None, compute_op=ALU.add)\
                                .then_inc(scattered, 16)

                pairs(pool, 0, EPAIRS, scatter)

            choose(pool, fast, general_path)

        @block.tensor
        def _(pe):
            def plan_count(c):
                pe.wait_ge(plan_onehots, 2 * c + 2)
                for e in range(c * ECOLS // PLAN_PARTS, (c + 1) * ECOLS // PLAN_PARTS):
                    mm = pe.matmul(ps_under, is_hi[:, e, :], under_lo[:, e, :],
                                   start=(e == 0), stop=(e == ECOLS - 1))
                mm.then_inc(plan_counted, 1)

            def plan_sum():
                pe.wait_ge(plan_under, 1)
                pe.matmul(ps_starts, ident[0:PLAN, 0:PLAN], under[:, 0:PLAN], start=True, stop=False)
                pe.matmul(ps_starts, before[:, :], under[:, PLAN:PLAN + 1].to_broadcast([PLAN, PLAN]),
                          start=False, stop=True).then_inc(plan_summed, 1)
                pe.wait_ge(faults_made, 2)
                for c in range(2):
                    mm = pe.matmul(ps_faults, faults[:, c:c + 1], ones[:, :], start=(c == 0), stop=(c == 1))
                mm.then_inc(faults_summed, 1)

            pe.wait_ge(s_const2, 3)
            pe.wait_ge(ids_moved, 1)
            for e in range(2):
                for u in range(U):
                    t = pe.transpose(ps_ends[e][:, u * EG:(u + 1) * EG],
                                     id_rows_f[:, e, :].rearrange("g (p u) -> g u p", u=U)[:, u, :],
                                     ident[0:EG, 0:EG])
            t.then_inc(ids_turned, 1)
            pe.wait_ge(s_halves, 2)
            pe.wait_ge(s_weights, 16 * NWEIGHTS)

            def turn_edges(i, s):
                g = 2 * i + s
                n = P
                pe.wait_ge(edges_in[s], 16 * i + 16)
                pe.wait_ge(gathered[s], 2 * U * 16 * (i + 1))
                if not (is_first(i) and s == 0):
                    pe.wait_ge(er_copied, g)
                    pe.wait_ge(s_copied, g)
                for u in range(U):
                    pe.transpose(ps_er[:, u * P:u * P + n], edge_recv[0:n, s, u, :], ident[0:n, 0:n])
                for v in range(2):
                    t = pe.transpose(ps_s[:, v * P:v * P + n], sender[0:n, s, v * P:(v + 1) * P], ident[0:n, 0:n])
                t.then_inc(e_turned, 1)

            def hide_edges(i, s):
                g = 2 * i + s
                n = P
                pe.wait_ge(er_copied, g + 1)
                pe.wait_ge(s_copied, g + 1)
                if not (is_first(i) and s == 0):
                    pe.wait_ge(e_relu, g)
                pe.matmul(cols(ps_eh[:, :], n), we1_er[:, :], cols(edge_recv_t[:, s, :], n), start=True, stop=False)
                for h in range(2):
                    mm = pe.matmul(ps_eh[:, :].rearrange("p (v h r) -> p h v r", v=2, h=2)[:, h, :, 0:n],
                                   we1_s[:, h, :],
                                   sender_t[:, s, :].rearrange("p (v r) -> p v r", v=2)[:, :, 0:n],
                                   start=False, stop=(h == 1))
                mm.then_inc(e_hidden, 1)

            def message_edges(i, s):
                g = 2 * i + s
                n = P
                pe.wait_ge(e_relu, g + 1)
                if not (is_first(i) and s == 0):
                    pe.wait_ge(rec_made, g)
                for u in range(U):
                    mm = pe.matmul(ps_msg[0:n, u * D:(u + 1) * D], ehid[:, s, u * P:u * P + n], we2_sb[:, :],
                                   start=True, stop=True)
                mm.then_inc(e_msg, 1)

            def turn_x(q, w, slot, first):
                if not first:
                    pe.wait_ge(node_copied, q)
                for u in range(U):
                    pe.transpose(ps_node[:, u * P:(u + 1) * P], xt[:, 2 * slot + w, u * D:(u + 2) * D], ident[:, :])

            def hide_nodes(q, w, first):
                pe.wait_ge(node_copied, q + 1)
                if not first:
                    pe.wait_ge(n_relu, q - 1)
                pe.matmul(ps_nh2[w][:, :], wn1_sb[:, :], node_t[:, w, :], start=True, stop=True)\
                  .then_inc(n_hidden, 1)

            def new_nodes(h, w, first):
                pe.wait_ge(n_relu, 2 * h + w + 1)
                if w == 0 and not first:
                    pe.wait_ge(n_added, h)
                for u in range(U):
                    mm = pe.matmul(ps_new[:, (w * U + u) * D:(w * U + u + 1) * D],
                                   nhid[:, w, u * P:(u + 1) * P], wn2_sb[:, :], start=True, stop=True)
                mm.then_inc(n_new, 1)

            def edge_group(i, s):
                turn_edges(i, s)
                hide_edges(i, s)
                message_edges(i, s)

            edge_group(0, 0)
            plan_count(0)
            edge_group(0, 1)
            plan_count(1)
            plan_count(2)
            edge_group(1, 0)
            plan_count(3)
            turn_edges(1, 1)
            plan_sum()
            hide_edges(1, 1)
            message_edges(1, 1)

            def fast():
                def turn_nodes(i, s, w):
                    h = 2 * i + s - LAG
                    q = 2 * h + w
                    if w == 0:
                        pe.wait_ge(low_made, h + 1)
                        pe.wait_ge(x_in[1 - s], 16 * (i - 2 + s + half_is(i, s, NPAIRS - 1)))
                        pe.wait_ge(onehot_made, h + 1)
                    turn_x(q, w, 1 - s, half_is(i, s, 0) and w == 0)
                    for b in range(U):
                        for part in (windows_hi, windows_lo):
                            mm = pe.matmul(ps_node[0:D, :].rearrange("p (u b r) -> p b u r", u=U, b=U)[:, b, :, :],
                                           part[:, 1 - s, U * w + b, :],
                                           onehot[:, 1 - s, U * w + b, :].rearrange("p (u r) -> p u r", u=U),
                                           start=(part is windows_hi), stop=(part is windows_lo))
                    mm.then_inc(n_turned, 1)

                def step(i):
                    for s in range(2):
                        h = 2 * i + s - LAG
                        first = half_is(i, s, 0)
                        edges_too, nodes_too = has_edges(i), has_half(i, s)
                        if edges_too:
                            turn_edges(i, s)
                        if has_half(i, s, -1):
                            new_nodes(h - 1, 1, False)
                        if nodes_too:
                            turn_nodes(i, s, 0)
                        if edges_too:
                            hide_edges(i, s)
                        if nodes_too:
                            turn_nodes(i, s, 1)
                            hide_nodes(2 * h, 0, first)
                        if edges_too:
                            message_edges(i, s)
                        if nodes_too:
                            hide_nodes(2 * h + 1, 1, first)
                            new_nodes(h, 0, first)

                fast_pairs(pe, step)

            def general_path():
                def edge_groups(i):
                    for s in range(2):
                        edge_group(i, s)

                pairs(pe, 2, EPAIRS, edge_groups)

                def sum_group(i):
                    for s in range(2):
                        n = eparts(i, s)
                        pe.wait_ge(rec_in[s], 16 * i + 16)
                        for u in range(U):
                            k = U * (2 * i + s) + u
                            began = not (is_first(i) and s == 0 and u == 0)
                            if began:
                                pe.wait_ge(same_made, k)
                            pe.matmul(ps_ids[:, 0:n], recin[0:n, s, u, D:D + 1].to_broadcast([n, P]),
                                      ident[0:n, 0:n], start=True, stop=True).then_inc(ids_spread, 1)
                            pe.wait_ge(same_made, k + 1)
                            if began:
                                pe.wait_ge(sum_copied, k)
                            pe.matmul(ps_sum[0:n, :], same[0:n, u % 2, 0:n], recin[0:n, s, u, 0:D],
                                      start=True, stop=True).then_inc(sum_made, 1)

                pairs(pe, 0, EPAIRS, sum_group)

                def node_halves(i):
                    for s in range(2):
                        h = 2 * i + s
                        pe.wait_ge(x_in[s], 32 * i + (64 if isinstance(i, int) and h == NPAIRS - 1 else 32))
                        for w in range(2):
                            turn_x(2 * h + w, w, s, is_first(i) and s == 0 and w == 0)
                            for u in range(U):
                                t = pe.transpose(ps_node[0:D, u * P:(u + 1) * P],
                                                 aggt[:, 2 * s + w, u * D:(u + 1) * D], ident[:, :])
                            t.then_inc(n_turned, 1)
                        for w in range(2):
                            hide_nodes(2 * h + w, w, is_first(i) and s == 0)
                        for w in range(2):
                            new_nodes(h, w, is_first(i) and s == 0)

                pairs(pe, 0, NPAIRS // 2, node_halves)

            choose(pe, fast, general_path)

        @block.scalar
        def _(act):
            def stage_ids(g, s, use):
                if not is_first(use):
                    act.wait_ge(gathered[s], 2 * U * 16 * use)
                act.activation(gather_ids[:, s, :, :],
                               end_ids[:, bass.ds(g, 1), :, :].rearrange("p g e u -> p (g e) u"), ACT.Copy)\
                   .then_inc(ids_staged, 1)

            def load_rows(i, s):
                g = 2 * i + s
                n = eparts(i, s)
                if not is_first(i):
                    act.wait_ge(e_turned, g - 1)
                act.dma_start(edge_recv[0:n, s, :, 0:D],
                             edges[bass.ds(g * GROUP, n * U), :].rearrange("(p u) d -> p u d", u=U))\
                  .then_inc(edges_in[s], 16)

            def copy_edges(i, s):
                g = 2 * i + s
                act.wait_ge(e_turned, g + 1)
                if not is_first(i):
                    act.wait_ge(e_hidden, g - 1)
                act.activation(sender_t[:, s, :], ps_s[:, 0:2 * P], ACT.Copy).then_inc(s_copied, 1)
                act.activation(edge_recv_t[:, s, :], ps_er[:, :], ACT.Copy).then_inc(er_copied, 1)

            def relu_edges(i, s):
                g = 2 * i + s
                act.wait_ge(e_hidden, g + 1)
                if not is_first(i):
                    act.wait_ge(e_msg, g - 1)
                act.activation(ehid[:, s, :], ps_eh[:, :], ACT.Relu, bias=be1_c[:, 0:1]).then_inc(e_relu, 1)

            def stage_ahead(i, s):
                if not isinstance(i, int) or 2 * i + s + 3 < EG:
                    stage_ids(2 * i + s + 3, 1 - s, i + 1 + s)

            def edge_groups(i):
                for s in range(2):
                    copy_edges(i, s)
                    relu_edges(i, s)
                    if has_edges(i + 1):
                        load_rows(i + 1, s)
                    stage_ahead(i, s)

            def copy_nodes(q, w, first):
                act.wait_ge(n_turned, q + 1)
                if not first:
                    act.wait_ge(n_hidden, q - 1)
                act.activation(node_t[:, w, :], ps_node[:, :], ACT.Copy).then_inc(node_copied, 1)

            def relu_nodes(q, w, first):
                act.wait_ge(n_hidden, q + 1)
                if not first:
                    act.wait_ge(n_new, q - 1)
                act.activation(nhid[:, w, :], ps_nh2[w][:, :], ACT.Relu, bias=bn1_c[:, 0:1]).then_inc(n_relu, 1)

            def store_half(h, slot):
                if is_last(h):
                    for w, n in ((0, P), (1, NTAIL)):
                        act.wait_ge(n_normed, h + w + 1)
                        act.dma_start(rows(out, 2 * h + w, n, D), res[0:n, 2 * slot + w, :]).then_inc(res_out[slot], 16)
                else:
                    act.wait_ge(n_normed, h + 1)
                    act.dma_start(rows_of_half(out, h), res[:, 2 * slot:2 * slot + 2, :]).then_inc(res_out[slot], 16)

            def root_nodes(h, first):
                act.wait_ge(n_aggr, h + 1)
                if not first:
                    act.wait_ge(n_rstd, h)
                act.activation(std[:, :], meanvar[:, :, 1], ACT.Sqrt, bias=eps[:, 0:1]).then_inc(n_std, 1)

            for e, t in enumerate((src, dst)):
                act.dma_start(end_ids[:, 0:FIRST_GROUPS, e, :],
                              t[0:FIRST_GROUPS * GROUP].rearrange("(g p u) -> p g u", p=P, u=U))\
                   .then_inc(first_ids_in, 16)
            act.wait_ge(s_const, 4)
            act.activation(warm[:, :], eps[:, :], ACT.Sqrt, bias=eps[:, 0:1]).then_inc(warmed, 1)
            act.wait_ge(first_ids_in, 32)
            for g in range(2):
                stage_ids(g, g, 0)
            for s in range(2):
                load_rows(0, s)
            act.wait_ge(ids_padded, 1)
            for e, t in enumerate((src, dst)):
                act.dma_start(id_rows[0:EG - 1, e, :], t[0:(EG - 1) * GROUP].rearrange("(g r) -> g r", r=GROUP))\
                   .then_inc(more_ids_in, 16)
                act.dma_start(id_rows[EG - 1:EG, e, 0:ETAIL * U],
                              t[(EG - 1) * GROUP:E].rearrange("(g r) -> g r", g=1)).then_inc(more_ids_in, 16)
            stage_ids(2, 0, 1)
            act.wait_ge(warmed, 1)
            act.wait_ge(s_weights, 16 * NWEIGHTS)
            edge_groups(0)
            act.wait_ge(ids_laid, 2)
            edge_groups(1)

            def fast():
                def halve_windows(h, slot, use):
                    act.wait_ge(windows_in[slot], 16 * BLOCKS * (use + 1))
                    if not is_first(use):
                        act.wait_ge(n_turned, 2 * h - 2)
                    act.activation(windows_hi[:, slot, :, :], windows[:, slot, :, 0:D], ACT.Copy)\
                       .then_inc(high_made, 1)

                def step(i):
                    for s in range(2):
                        h = 2 * i + s - LAG
                        first = half_is(i, s, 0)
                        edges_too, nodes_too = has_edges(i), has_half(i, s)
                        if edges_too:
                            copy_edges(i, s)
                        if nodes_too:
                            copy_nodes(2 * h, 0, first)
                        if s == 1 and edges_too:
                            store_rec(act, i, 0)
                        if s == 0 and has_edges(i - 1):
                            store_rec(act, i - 1, 1)
                        if edges_too:
                            relu_edges(i, s)
                        if has_edges(i + 1):
                            load_rows(i + 1, s)
                        if nodes_too:
                            copy_nodes(2 * h + 1, 1, first)
                        if has_half(i, s, -1):
                            root_nodes(h - 1, half_is(i, s, 1))
                        if has_half(i, s, 1):
                            halve_windows(h + 1, s, i - 2)
                        if nodes_too:
                            relu_nodes(2 * h, 0, first)
                            relu_nodes(2 * h + 1, 1, first)
                        if has_half(i, s, -2):
                            store_half(h - 2, 1 - s)
                        if edges_too:
                            stage_ahead(i, s)

                fast_pairs(act, step, ahead=1, behind=1)
                for h in range(2 * LAST - LAG, NPAIRS):
                    store_half(h, h % 2)

            def general_path():
                with act.Fori(2, EPAIRS - 2) as i:
                    edge_groups(i)
                for i in range(EPAIRS - 2, EPAIRS):
                    edge_groups(i)

                def sum_group(i):
                    for s in range(2):
                        n = eparts(i, s)
                        for u in range(U):
                            k = U * (2 * i + s) + u
                            act.wait_ge(sum_made, k + 1)
                            if not (is_first(i) and s == 0 and u < 2):
                                act.wait_ge(scattered, 16 * (k - 1))
                            act.activation(summed[0:n, u % 2, :], ps_sum[0:n, :], ACT.Copy).then_inc(sum_copied, 1)

                pairs(act, 0, EPAIRS, sum_group)

                def node_halves(i):
                    for s in range(2):
                        h = 2 * i + s
                        first = is_first(i) and s == 0
                        for w in range(2):
                            copy_nodes(2 * h + w, w, first)
                        for w in range(2):
                            relu_nodes(2 * h + w, w, first)
                        root_nodes(h, first)
                        store_half(h, s)

                pairs(act, 0, NPAIRS // 2, node_halves)

            choose(act, fast, general_path)
            act.wait_ge(res_out[0], 16 * (NPAIRS // 2))
            act.wait_ge(res_out[1], 16 * (NPAIRS // 2) + 16)

        @block.vector
        def _(dve):
            dve.memset(dstp[:, ECOLS:ECOLS + 1], PLAN * PLAN * P).then_inc(plan_edge, 1)
            dve.memset(before[:, :], 1.0).then_inc(plan_edge, 1)
            dve.memset(we1_s[D:2 * D, 0, :], 0.0).then_inc(s_halves, 1)
            dve.memset(we1_s[0:D, 1, :], 0.0).then_inc(s_halves, 1)
            dve.memset(id_rows[:, :, ETAIL * U:GROUP], 0).then_inc(ids_padded, 1)
            dve.memset(no_message[:, :, :], 0.0).then_inc(plan_step, 1)
            dve.memset(faults[:, :], 0.0).then_inc(plan_step, 1)
            dve.memset(ones[:, :], 1.0).then_inc(plan_step, 1)
            dve.wait_ge(plan_step, 3)
            dve.memset(no_message[:, :, D:REC], -1.0).then_inc(pad_made, 1)
            dve.wait_ge(plan_iota, 5)
            dve.tensor_copy(count_to[:, :], count_i[:, :]).then_inc(plan_step, 1)
            dve.tensor_copy(place[:, :], place_i[:, :]).then_inc(placed, 1)
            dve.tensor_copy(half_base[:, :], half_base_i[:, :]).then_inc(base_moved, 1)
            dve.tensor_copy(spare[:, :], row_id[:, 0:1]).then_inc(placed, 1)
            dve.wait_ge(plan_in, 32)
            dve.tensor_scalar(blk_hi[:, :], dstp[:, 0:ECOLS], (P * PLAN).bit_length() - 1, None,
                              ALU.arith_shift_right).then_inc(plan_step, 1)
            dve.tensor_scalar(blk_lo[:, :], dstp[:, 0:ECOLS], P.bit_length() - 1, PLAN - 1,
                              ALU.arith_shift_right, ALU.bitwise_and).then_inc(plan_step, 1)
            dve.tensor_tensor(in_order[:, :], dstp[:, 0:ECOLS], dstp[:, 1:ECOLS + 1], ALU.is_gt)\
               .then_inc(plan_step, 1)
            dve.wait_ge(plan_step, 7)
            dve.tensor_copy(hi16[:, :], blk_hi[:, :]).then_inc(plan_step, 1)
            dve.tensor_copy(lo16[:, :], blk_lo[:, :]).then_inc(plan_step, 1)
            dve.tensor_reduce(faults[0:EROWS, 0:1], in_order[:, :], AX_X, ALU.max).then_inc(faults_made, 1)
            dve.wait_ge(plan_step, 9)

            def plan_onehot(c):
                n = ECOLS // PLAN_PARTS
                e = slice(c * n, (c + 1) * n)
                dve.tensor_tensor(is_hi[:, e, :], hi16[:, e].unsqueeze(2).to_broadcast([EROWS, n, PLAN]),
                                  count_to[:, 0:PLAN].unsqueeze(1).to_broadcast([EROWS, n, PLAN]), ALU.is_equal)\
                   .then_inc(plan_onehots, 1)
                dve.tensor_tensor(under_lo[:, e, :], lo16[:, e].unsqueeze(2).to_broadcast([EROWS, n, PLAN + 1]),
                                  count_to[:, :].unsqueeze(1).to_broadcast([EROWS, n, PLAN + 1]), ALU.is_lt)\
                   .then_inc(plan_onehots, 1)

            def note_receivers(i, s):
                if not is_first(i):
                    dve.wait_ge(rec_out[s], 16 * i)
                dve.tensor_copy(rec[:, s, :, D:D + 2],
                                end_ids[:, bass.ds(2 * i + s, 1), 1, :].rearrange("p g u -> p (g u)")
                                .unsqueeze(2).to_broadcast([P, U, 2])).then_inc(dst_noted, 1)

            def make_rec(i, s):
                dve.wait_ge(e_msg, 2 * i + s + 1)
                dve.tensor_tensor(rec[:, s, :, 0:D], ps_msg[:, 0:U * D].rearrange("p (u d) -> p u d", u=U),
                                  be2_b[:, :].unsqueeze(1).to_broadcast([P, U, D]), ALU.add)\
                   .then_inc(rec_made, 1)

            def edge_groups(i):
                for s in range(2):
                    note_receivers(i, s)
                    make_rec(i, s)

            plan_onehot(0)
            dve.wait_ge(more_ids_in, 64)
            dve.tensor_copy(id_rows_f[:, :, :], id_rows[:, :, :]).then_inc(ids_moved, 1)
            dve.wait_ge(first_ids_in, 32)
            note_receivers(0, 0)
            note_receivers(0, 1)
            dve.wait_ge(ids_turned, 1)
            for e in range(2):
                dve.tensor_copy(end_ids[:, FIRST_GROUPS:EG, e, :],
                                ps_ends[e][:, 0:U * EG].rearrange("p (u g) -> p g u", u=U)[:, FIRST_GROUPS:EG, :])\
                   .then_inc(ids_laid, 1)
            plan_onehot(1)
            plan_onehot(2)
            dve.wait_ge(s_weights, 16 * NWEIGHTS)
            make_rec(0, 0)
            plan_onehot(3)
            make_rec(0, 1)
            note_receivers(1, 0)
            make_rec(1, 0)
            note_receivers(1, 1)
            dve.wait_ge(plan_counted, PLAN_PARTS)
            dve.tensor_copy(under[:, :], ps_under).then_inc(plan_under, 1)
            dve.wait_ge(plan_under, 1)
            dve.tensor_tensor(over[:, 0, :], under[:, 1:PLAN + 1], under[:, 0:PLAN], ALU.subtract).then_inc(plan_step, 1)
            dve.wait_ge(plan_summed, 1)
            dve.tensor_copy(starts_sb[:, :], ps_starts).then_inc(starts_made, 1)
            dve.tensor_tensor(over[:, 1, :], ps_starts, limit[:, :], ALU.subtract).then_inc(plan_step, 1)
            dve.wait_ge(plan_step, 11)
            dve.tensor_reduce(worst[:, :], over[:, :, :], AX_X, ALU.max).then_inc(plan_step, 1)
            dve.wait_ge(plan_step, 12)
            dve.tensor_scalar(worst_over[:, 0:1], worst[:, 0:1], float(BLOCK_EDGES), None, ALU.is_gt)\
               .then_inc(plan_step, 1)
            dve.tensor_scalar(worst_over[:, 1:2], worst[:, 1:2], 0.0, None, ALU.is_gt).then_inc(plan_step, 1)
            dve.wait_ge(plan_step, 14)
            dve.tensor_tensor(faults[0:PLAN, 1:2], worst_over[:, 0:1], worst_over[:, 1:2], ALU.max)\
               .then_inc(faults_made, 1)
            dve.wait_ge(faults_summed, 1)
            dve.tensor_scalar(general[:, :], ps_faults, 1.0, None, ALU.min).then_inc(plan_ready, 1)
            make_rec(1, 1)

            def add_nodes(h, slot, first):
                by_row = y[:, :, :].rearrange("p w (u d) -> p (w u) d", u=U)
                dve.wait_ge(n_new, 2 * h + 2)
                if not first:
                    dve.wait_ge(n_centered, h)
                dve.tensor_tensor(y[:, :, :], ps_new[:, :].rearrange("p (w c) -> p w c", w=2),
                                  xt[:, 2 * slot:2 * slot + 2, D:(U + 1) * D], ALU.add).then_inc(n_added, 1)
                dve.wait_ge(n_added, h + 1)
                dve.tensor_tensor(by_row, by_row, bn2_b[:, :].unsqueeze(1).to_broadcast([P, 2 * U, D]), ALU.add)\
                   .then_inc(n_biased, 1)
                dve.wait_ge(n_biased, h + 1)
                for u in range(2 * U):
                    st = dve.bn_stats(stats[:, u, :], by_row[:, u, :])
                st.then_inc(n_stats, 1)
                dve.wait_ge(n_stats, h + 1)
                if not first:
                    dve.wait_ge(n_std, h)
                dve.sem_inc(dve_passed, 1)
                for u in range(2 * U):
                    ag = dve.bn_aggr(meanvar[:, u, :], stats[:, u, :])
                ag.then_inc(n_aggr, 1)

            def norm_nodes(h, slot, use):
                by_row = y[:, :, :].rearrange("p w (u d) -> p (w u) d", u=U)
                result = res[:, 2 * slot:2 * slot + 2, :].rearrange("p w (u d) -> p (w u) d", u=U)
                if not is_first(use):
                    dve.wait_ge(res_out[slot], 16 * use)
                dve.wait_ge(n_aggr, h + 1)
                dve.tensor_tensor(result, by_row, meanvar[:, :, 0:1].to_broadcast([P, 2 * U, D]), ALU.subtract)\
                   .then_inc(n_centered, 1)
                dve.wait_ge(n_std, h + 1)
                dve.reciprocal(rstd[:, :], std[:, :]).then_inc(n_rstd, 1)
                dve.wait_ge(n_centered, h + 1)
                dve.wait_ge(n_rstd, h + 1)
                parts = 2 if is_last(h) else 1
                for k in range(parts):
                    r = slice(k * 2 * U // parts, (k + 1) * 2 * U // parts)
                    n = 2 * U // parts
                    dve.tensor_tensor(result[:, r, :], result[:, r, :],
                                      rstd[:, r].unsqueeze(2).to_broadcast([P, n, D]), ALU.mult)\
                       .then_inc(n_normed, 1)

            def fast():
                def make_onehots(h, slot, use):
                    dve.wait_ge(windows_in[slot], 16 * BLOCKS * (use + 1))
                    dve.wait_ge(base_moved, h + 1)
                    if not is_first(use):
                        dve.wait_ge(n_turned, 2 * h - 2)
                    dve.tensor_tensor(in_block[:, slot, :], windows[:, slot, :, D], half_base[:, :], ALU.subtract)\
                       .then_inc(placed, 1)
                    dve.wait_ge(placed, h + 3)
                    dve.tensor_scalar(half_base[:, :], half_base[:, :], float(HALF), None, ALU.add)\
                       .then_inc(base_moved, 1)
                    dve.tensor_tensor(onehot[:, slot, :, :], place[:, :].unsqueeze(1).to_broadcast([P, BLOCKS, P]),
                                      in_block[:, slot, :].unsqueeze(2).to_broadcast([P, BLOCKS, P]), ALU.is_equal)\
                       .then_inc(onehot_made, 1)

                def make_low(h, slot, use):
                    dve.wait_ge(high_made, h + 1)
                    dve.wait_ge(windows_in[slot], 16 * BLOCKS * (use + 1))
                    if not is_first(use):
                        dve.wait_ge(n_turned, 2 * h - 2)
                    dve.tensor_tensor(windows_lo[:, slot, :, :], windows[:, slot, :, 0:D], windows_hi[:, slot, :, :],
                                      ALU.subtract).then_inc(low_made, 1)

                dve.wait_ge(placed, 2)

                def step(i):
                    for s in range(2):
                        h = 2 * i + s - LAG
                        if has_edges(i):
                            note_receivers(i, s)
                        if has_half(i, s, -1):
                            add_nodes(h - 1, s, half_is(i, s, 1))
                        if has_half(i, s, 1):
                            make_onehots(h + 1, s, i - 2)
                            make_low(h + 1, s, i - 2)
                        if has_half(i, s, -1):
                            norm_nodes(h - 1, s, i - 3)
                        if has_edges(i):
                            make_rec(i, s)

                fast_pairs(dve, step, behind=1)

            def general_path():
                dve.memset(zeros[:, :], 0.0).then_inc(zeros_made, 1)
                pairs(dve, 2, EPAIRS, edge_groups)

                def sum_group(i):
                    for s in range(2):
                        n = eparts(i, s)
                        for u in range(U):
                            k = U * (2 * i + s) + u
                            b = u % 2
                            began2 = not (is_first(i) and s == 0 and u < 2)
                            began = not (is_first(i) and s == 0 and u == 0)
                            receiver = recin[0:n, s, u, D:D + 1]
                            if u == 0:
                                dve.wait_ge(rec_in[s], 16 * i + 16)
                            dve.wait_ge(ids_spread, k + 1)
                            if began2:
                                dve.wait_ge(sum_made, k - 1)
                            dve.tensor_scalar(same[0:n, b, 0:n], ps_ids[0:n, 0:n], receiver, None, ALU.is_equal)\
                               .then_inc(same_made, 1)
                            dve.wait_ge(same_made, k + 1)
                            if began:
                                dve.wait_ge(later_made, k)
                            dve.tensor_tensor_reduce(same_earlier[0:n, 0:n], same[0:n, b, 0:n], earlier[0:n, 0:n],
                                                     1.0, 0.0, ALU.mult, ALU.add, n_earlier[0:n, b:b + 1])\
                               .then_inc(counted, 1)
                            dve.wait_ge(counted, k + 1)
                            if began:
                                dve.wait_ge(row_made, k)
                            dve.tensor_scalar(is_later[0:n, b:b + 1], n_earlier[0:n, b:b + 1], 1.0, None, ALU.min)\
                               .then_inc(later_made, 1)
                            dve.tensor_tensor(to_spare[0:n, b:b + 1], spare[0:n, :], receiver, ALU.subtract)\
                               .then_inc(spare_made, 1)
                            dve.wait_ge(later_made, k + 1)
                            dve.wait_ge(spare_made, k + 1)
                            if began2:
                                dve.wait_ge(scattered, 16 * (k - 1))
                            dve.scalar_tensor_tensor(out=row_id[0:n, b:b + 1], in0=to_spare[0:n, b:b + 1],
                                                     scalar=is_later[0:n, b:b + 1], in1=receiver,
                                                     op0=ALU.mult, op1=ALU.add).then_inc(row_made, 1)

                dve.wait_ge(placed, 2)
                pairs(dve, 0, EPAIRS, sum_group)

                def node_halves(i):
                    for s in range(2):
                        add_nodes(2 * i + s, s, is_first(i) and s == 0)
                        norm_nodes(2 * i + s, s, i)

                pairs(dve, 0, NPAIRS // 2, node_halves)

            choose(dve, fast, general_path)


_INS = ['x', 'src', 'dst', 'edge_attr_64', 'L0_gnn_We1', 'L0_gnn_be1', 'L0_gnn_We2', 'L0_gnn_be2',
        'L0_gnn_Wn1', 'L0_gnn_bn1', 'L0_gnn_Wn2', 'L0_gnn_bn2']


def kernel(**inputs):
    import numpy as _np
    import concourse.bacc as _bacc
    from concourse import mybir as _mybir
    from concourse.bass_utils import run_bass_kernel_spmd as _run

    nc = _bacc.Bacc("TRN2", target_bir_lowering=False, num_devices=1)
    arrays, args = {}, []
    for name in _INS:
        a = _np.ascontiguousarray(inputs[name])
        arrays[f"in_{name}"] = a
        args.append(nc.dram_tensor(f"in_{name}", a.shape, _mybir.dt.from_np(a.dtype), kind="ExternalInput").ap())
    out = nc.dram_tensor("out_0", inputs['x'].shape, F32, kind="ExternalOutput").ap()
    gnn_resnorm(nc, *args, out)
    r = _run(nc, [arrays], core_ids=[0])
    return r.results[0]["out_0"]
```
